# Optimizing a Trainium2 kernel written in Bass

```python
import numpy as np
import jax
import jax.numpy as jnp

def _softmax(x, axis=-1):
    return jax.nn.softmax(x, axis=axis)

def _gelu(x):
    return jax.nn.gelu(x, approximate=True)

def _silu(x):
    return jax.nn.silu(x)

def _sigmoid(x):
    return jax.nn.sigmoid(x)

def _layernorm(x, axis=-1, eps=1e-05):
    m = jnp.mean(x, axis=axis, keepdims=True)
    v = jnp.var(x, axis=axis, keepdims=True)
    return (x - m) / jnp.sqrt(v + eps)

def _scatter_add(tgt, idx, src, axis=0):
    return tgt.at[idx].add(src)

def _segment_sum(src, seg, n):
    return jax.ops.segment_sum(src, seg, n)
kernel_name = 'mk_perceiver_d1_seqx_r2_7e8c6c'

def setup_inputs(seed: int=0):
    np.random.seed(seed)
    _w = jnp.asarray

    def _rec_inputs():
        import jax
        import jax.numpy as jnp
        _rk = jax.random.key(seed)
        x = 7.22e-05 + 1 * jax.random.normal(jax.random.fold_in(_rk, 1), (4, 128, 1024), jnp.float32)
        _lenS = 128 - jax.random.randint(jax.random.fold_in(_rk, 7), (4,), 0, max(1, 128 // 4) + 1, jnp.int32)
        _lenS2 = 2048 - jax.random.randint(jax.random.fold_in(_rk, 8), (4,), 0, max(1, 2048 // 4) + 1, jnp.int32)
        _ctx_2048P = jax.random.normal(jax.random.fold_in(_rk, 11), (4, 16, 1024), jnp.float32)
        _ctx_2048c = jax.random.dirichlet(jax.random.fold_in(_rk, 511), 0.3 * jnp.ones((16,), jnp.float32), (4, 2048))
        _ctx_2048t = jnp.einsum('bsk,bkd->bsd', _ctx_2048c, _ctx_2048P)
        _ctx_2048t = _ctx_2048t * jax.lax.rsqrt(jnp.mean(jnp.square(_ctx_2048t)) + 1e-12) * 0.953939
        ctx_2048 = -0.000514642 + 1.00011 * (_ctx_2048t + 0.3 * jax.random.normal(jax.random.fold_in(_rk, 611), (4, 2048, 1024), jnp.float32))
        return (x, ctx_2048)
    x, ctx_2048 = _rec_inputs()

    def _L0_xattn_setup():
        import jax, jax.numpy as jnp
        import numpy as np
        D_MODEL = 1024
        NUM_HEADS = 16
        HEAD_DIM = D_MODEL // NUM_HEADS

        def _fq_sym(x, axis):
            s = jnp.max(jnp.abs(x), axis=axis, keepdims=True) / 127.0
            s = jnp.maximum(s, 1e-08)
            q = jnp.clip(jnp.round(x / s), -127.0, 127.0) * s
            return x + jax.lax.stop_gradient(q - x)

        def _fq_unsigned(x, axis):
            s = jnp.max(x, axis=axis, keepdims=True) / 255.0
            s = jnp.maximum(s, 1e-08)
            q = jnp.clip(jnp.round(x / s), 0.0, 255.0) * s
            return x + jax.lax.stop_gradient(q - x)
        key = jax.random.key(seed)
        ks = jax.random.split(key, 8)
        B, N, M, C = (2, 1024, 256, D_MODEL)
        return {'x': jax.random.normal(ks[0], (B, N, C), jnp.float32), 'cond': jax.random.normal(ks[1], (B, M, C), jnp.float32), 'Wq': jax.random.normal(ks[2], (C, C), jnp.float32) * 0.02, 'bq': jnp.zeros((C,), jnp.float32), 'Wkv': jax.random.normal(ks[3], (C, 2 * C), jnp.float32) * 0.02, 'bkv': jnp.zeros((2 * C,), jnp.float32), 'Wp': jax.random.normal(ks[4], (C, C), jnp.float32) * 0.02, 'bp': jnp.zeros((C,), jnp.float32)}
    _L0_xattn_all = _L0_xattn_setup()
    _L0_xattn_in = {k: v for k, v in _L0_xattn_all.items() if k in ('Wq', 'bq', 'Wkv', 'bkv', 'Wp', 'bp')}
    del _L0_xattn_all

    def _L0_attn_setup():
        import jax, jax.numpy as jnp
        import numpy as np
        N_HEADS = 16

        def _rope_tables(seq_len, head_dim, dtype=jnp.float32):
            pos = jnp.arange(seq_len, dtype=jnp.float32)[:, None]
            exps = -jnp.arange(0, head_dim, 2, dtype=jnp.float32) / head_dim
            thetas = jnp.repeat(jnp.power(10000.0, exps), 2)
            angles = pos * thetas[None, :]
            return (jnp.cos(angles).astype(dtype), jnp.sin(angles).astype(dtype))

        def _apply_rope(x, cos, sin):
            x_even = x[..., 0::2]
            x_odd = x[..., 1::2]
            x_rot = jnp.stack((-x_odd, x_even), axis=-1).reshape(x.shape)
            return x * cos[None, :, None, :] + x_rot * sin[None, :, None, :]
        key = jax.random.key(seed)
        ks = jax.random.split(key, 5)
        B, S, E = (2, 1024, 1024)
        scale = 1.0 / np.sqrt(E)
        return {'x': jax.random.normal(ks[0], (B, S, E), dtype=jnp.float32), 'Wq': jax.random.normal(ks[1], (E, E), dtype=jnp.float32) * scale, 'bq': jnp.zeros((E,), dtype=jnp.float32), 'Wk': jax.random.normal(ks[2], (E, E), dtype=jnp.float32) * scale, 'bk': jnp.zeros((E,), dtype=jnp.float32), 'Wv': jax.random.normal(ks[3], (E, E), dtype=jnp.float32) * scale, 'bv': jnp.zeros((E,), dtype=jnp.float32), 'Wo': jax.random.normal(ks[4], (E, E), dtype=jnp.float32) * scale, 'bo': jnp.zeros((E,), dtype=jnp.float32)}
    _L0_attn_all = _L0_attn_setup()
    _L0_attn_in = {k: v for k, v in _L0_attn_all.items() if k in ('Wq', 'bq', 'Wk', 'bk', 'Wv', 'bv', 'Wo', 'bo')}
    del _L0_attn_all

    def _L0_ffn_setup():
        import jax, jax.numpy as jnp
        import numpy as np
        _FP4_LUT = jnp.array([0.0, 0.5, 1.0, 1.5, 2.0, 3.0, 4.0, 6.0, -0.0, -0.5, -1.0, -1.5, -2.0, -3.0, -4.0, -6.0], dtype=jnp.float32)
        GROUP_SIZE = 128
        EPS = 1e-06

        def _dequant_fp4(packed_i32, scales_f16, group_size):
            out_f, in_p = packed_i32.shape
            w = packed_i32.astype(jnp.uint32)
            shifts = jnp.arange(8, dtype=jnp.uint32) * 4
            nib = w[:, :, None] >> shifts & jnp.uint32(15)
            vals = _FP4_LUT[nib.astype(jnp.int32)].reshape(out_f, in_p * 8)
            s = scales_f16.astype(jnp.float32).T
            s_full = jnp.repeat(s, group_size, axis=1)
            return vals * s_full
        key = jax.random.key(seed)
        k1, k2, k3, k4, k5 = jax.random.split(key, 5)
        B, S, H, I = (4, 1024, 1024, 2816)
        x = jax.random.normal(k1, (B, S, H), dtype=jnp.float32)
        gate_up_packed = jax.random.randint(k2, (2 * I, H // 8), 0, 2147483647, dtype=jnp.int32)
        gate_up_scales = jax.random.uniform(k3, (H // GROUP_SIZE, 2 * I), dtype=jnp.float32).astype(jnp.float16)
        down_packed = jax.random.randint(k4, (H, I // 8), 0, 2147483647, dtype=jnp.int32)
        down_scales = jax.random.uniform(k5, (I // GROUP_SIZE, H), dtype=jnp.float32).astype(jnp.float16)
        return {'x': x, 'gate_up_packed': gate_up_packed, 'gate_up_scales': gate_up_scales, 'down_packed': down_packed, 'down_scales': down_scales}
    _L0_ffn_all = _L0_ffn_setup()
    _L0_ffn_in = {k: v for k, v in _L0_ffn_all.items() if k in ('gate_up_packed', 'gate_up_scales', 'down_packed', 'down_scales')}
    del _L0_ffn_all
    return {'x': x, 'ctx_2048': ctx_2048, 'L0_xattn_Wq': _L0_xattn_in['Wq'], 'L0_xattn_bq': _L0_xattn_in['bq'], 'L0_xattn_Wkv': _L0_xattn_in['Wkv'], 'L0_xattn_bkv': _L0_xattn_in['bkv'], 'L0_xattn_Wp': _L0_xattn_in['Wp'], 'L0_xattn_bp': _L0_xattn_in['bp'], 'L0_attn_Wq': _L0_attn_in['Wq'], 'L0_attn_bq': _L0_attn_in['bq'], 'L0_attn_Wk': _L0_attn_in['Wk'], 'L0_attn_bk': _L0_attn_in['bk'], 'L0_attn_Wv': _L0_attn_in['Wv'], 'L0_attn_bv': _L0_attn_in['bv'], 'L0_attn_Wo': _L0_attn_in['Wo'], 'L0_attn_bo': _L0_attn_in['bo'], 'L0_ffn_gate_up_packed': _L0_ffn_in['gate_up_packed'], 'L0_ffn_gate_up_scales': _L0_ffn_in['gate_up_scales'], 'L0_ffn_down_packed': _L0_ffn_in['down_packed'], 'L0_ffn_down_scales': _L0_ffn_in['down_scales']}

def reference(x, ctx_2048, L0_xattn_Wq, L0_xattn_bq, L0_xattn_Wkv, L0_xattn_bkv, L0_xattn_Wp, L0_xattn_bp, L0_attn_Wq, L0_attn_bq, L0_attn_Wk, L0_attn_bk, L0_attn_Wv, L0_attn_bv, L0_attn_Wo, L0_attn_bo, L0_ffn_gate_up_packed, L0_ffn_gate_up_scales, L0_ffn_down_packed, L0_ffn_down_scales):
    import jax
    import jax.numpy as jnp

    def _L0_xattn_ref(x, cond, Wq, bq, Wkv, bkv, Wp, bp):
        import jax, jax.numpy as jnp
        import numpy as np
        D_MODEL = 1024
        NUM_HEADS = 16
        HEAD_DIM = D_MODEL // NUM_HEADS

        def _fq_sym(x, axis):
            s = jnp.max(jnp.abs(x), axis=axis, keepdims=True) / 127.0
            s = jnp.maximum(s, 1e-08)
            q = jnp.clip(jnp.round(x / s), -127.0, 127.0) * s
            return x + jax.lax.stop_gradient(q - x)

        def _fq_unsigned(x, axis):
            s = jnp.max(x, axis=axis, keepdims=True) / 255.0
            s = jnp.maximum(s, 1e-08)
            q = jnp.clip(jnp.round(x / s), 0.0, 255.0) * s
            return x + jax.lax.stop_gradient(q - x)
        B, N, C = x.shape
        H, hd = (NUM_HEADS, HEAD_DIM)
        q = (x @ Wq + bq).reshape(1, B * N, H, hd)
        kv = (cond @ Wkv + bkv).reshape(1, -1, 2, H, hd)
        k, v = (kv[:, :, 0], kv[:, :, 1])
        scale = 1.0 / np.sqrt(hd).astype(np.float32)
        q = jnp.transpose(q * scale, (0, 2, 1, 3))
        k = jnp.transpose(k, (0, 2, 1, 3))
        v = jnp.transpose(v, (0, 2, 1, 3))
        q = _fq_sym(q, axis=-1)
        k = _fq_sym(k, axis=-1)
        v = _fq_sym(v, axis=2)
        attn = jnp.einsum('bhqd,bhkd->bhqk', q, k)
        attn = jax.nn.softmax(attn.astype(jnp.float32), axis=-1)
        attn = _fq_unsigned(attn, axis=-1)
        out = jnp.einsum('bhqk,bhkd->bhqd', attn, v)
        out = jnp.transpose(out, (0, 2, 1, 3)).reshape(B, N, C)
        return out @ Wp + bp

    def _L0_attn_ref(x, Wq, bq, Wk, bk, Wv, bv, Wo, bo):
        import jax, jax.numpy as jnp
        import numpy as np
        N_HEADS = 16

        def _rope_tables(seq_len, head_dim, dtype=jnp.float32):
            pos = jnp.arange(seq_len, dtype=jnp.float32)[:, None]
            exps = -jnp.arange(0, head_dim, 2, dtype=jnp.float32) / head_dim
            thetas = jnp.repeat(jnp.power(10000.0, exps), 2)
            angles = pos * thetas[None, :]
            return (jnp.cos(angles).astype(dtype), jnp.sin(angles).astype(dtype))

        def _apply_rope(x, cos, sin):
            x_even = x[..., 0::2]
            x_odd = x[..., 1::2]
            x_rot = jnp.stack((-x_odd, x_even), axis=-1).reshape(x.shape)
            return x * cos[None, :, None, :] + x_rot * sin[None, :, None, :]
        B, S, E = x.shape
        H = N_HEADS
        D = E // H
        cos, sin = _rope_tables(S, D, x.dtype)
        q = (x @ Wq + bq).reshape(B, S, H, D)
        k = (x @ Wk + bk).reshape(B, S, H, D)
        v = (x @ Wv + bv).reshape(B, S, H, D)
        q = _apply_rope(q, cos, sin)
        k = _apply_rope(k, cos, sin)
        scores = jnp.einsum('bshd,bthd->bhst', q, k) / jnp.sqrt(jnp.asarray(D, x.dtype))
        causal = jnp.triu(jnp.ones((S, S), dtype=bool), k=1)
        scores = jnp.where(causal[None, None], -jnp.inf, scores)
        attn = jax.nn.softmax(scores, axis=-1)
        out = jnp.einsum('bhst,bthd->bshd', attn, v).reshape(B, S, E)
        return out @ Wo + bo

    def _L0_ffn_ref(x, gate_up_packed, gate_up_scales, down_packed, down_scales):
        import jax, jax.numpy as jnp
        import numpy as np
        _FP4_LUT = jnp.array([0.0, 0.5, 1.0, 1.5, 2.0, 3.0, 4.0, 6.0, -0.0, -0.5, -1.0, -1.5, -2.0, -3.0, -4.0, -6.0], dtype=jnp.float32)
        GROUP_SIZE = 128
        EPS = 1e-06

        def _dequant_fp4(packed_i32, scales_f16, group_size):
            out_f, in_p = packed_i32.shape
            w = packed_i32.astype(jnp.uint32)
            shifts = jnp.arange(8, dtype=jnp.uint32) * 4
            nib = w[:, :, None] >> shifts & jnp.uint32(15)
            vals = _FP4_LUT[nib.astype(jnp.int32)].reshape(out_f, in_p * 8)
            s = scales_f16.astype(jnp.float32).T
            s_full = jnp.repeat(s, group_size, axis=1)
            return vals * s_full
        I = gate_up_packed.shape[0] // 2
        w_gu = _dequant_fp4(gate_up_packed, gate_up_scales, GROUP_SIZE)
        w_down = _dequant_fp4(down_packed, down_scales, GROUP_SIZE)
        gate_up = jnp.einsum('bsh,oh->bso', x, w_gu)
        gate, up = (gate_up[..., :I], gate_up[..., I:])
        h = jax.nn.silu(gate) * up
        y = jnp.einsum('bsi,hi->bsh', h, w_down)
        rms = jnp.sqrt(jnp.mean(y * y, axis=-1, keepdims=True) + EPS)
        return y / rms
    x = x + _L0_xattn_ref(_layernorm(x, axis=-1), ctx_2048, L0_xattn_Wq, L0_xattn_bq, L0_xattn_Wkv, L0_xattn_bkv, L0_xattn_Wp, L0_xattn_bp)
    x = x + _L0_attn_ref(_layernorm(x, axis=-1), L0_attn_Wq, L0_attn_bq, L0_attn_Wk, L0_attn_bk, L0_attn_Wv, L0_attn_bv, L0_attn_Wo, L0_attn_bo)
    x = x + _L0_ffn_ref(_layernorm(x, axis=-1), L0_ffn_gate_up_packed, L0_ffn_gate_up_scales, L0_ffn_down_packed, L0_ffn_down_scales)
    return x

_drawn_inputs = setup_inputs


def setup_inputs(seed=0):
    import zlib

    import numpy as np

    out = dict(_drawn_inputs(seed))
    spreads = {'L0_xattn_bq': (0.0, 0.8),
     'L0_xattn_bkv': (0.0, 0.1),
     'L0_xattn_bp': (0.0, 0.1),
     'L0_attn_bq': (0.0, 0.329),
     'L0_attn_bk': (0.0, 0.633),
     'L0_attn_bv': (0.0, 0.1),
     'L0_attn_bo': (0.0, 0.1)}
    factors = {}
    for name, (base, spread) in spreads.items():
        noise = np.random.default_rng([zlib.crc32(name.encode()), seed]).standard_normal(out[name].shape)
        drawn = base * np.exp(spread * noise) if base else spread * noise
        out[name] = jnp.asarray(drawn.astype(out[name].dtype))
    for name, factor in factors.items():
        out[name] = (out[name] * factor).astype(out[name].dtype)
    return out
```

```python
from contextlib import ExitStack

import numpy as np

import concourse.bass as bass
from concourse import mybir

ALU = mybir.AluOpType
ACT = mybir.ActivationFunctionType
AX = mybir.AxisListType
F32 = mybir.dt.float32
F16 = mybir.dt.float16
U16 = mybir.dt.uint16
I32 = mybir.dt.int32

P = 128
B, S, D = 4, 128, 1024
T = B * S // P
HEADS, HD = 16, 64
KD = D // P
HALF = 512
NKV = 4 * 2048
KVT = NKV // P
X_SCALE, W_SCALE, K_SCALE = 16.0, 256.0, 64.0
UNSCALE = 1.0 / (X_SCALE * W_SCALE)
MAGIC = 1.5 * 2.0 ** 23
LEVELS = 127.0
LN_EPS, RMS_EPS = 1e-5, 1e-6
INNER = 2816
WORD = 8
NB = 3
LAST = (INNER - 2 * D) // WORD
GROUP_ROWS = 16
SC_SCALE = 4096.0
NIB_SCALE = 2.0 ** -14
H_SCALE = 2.0 ** -10


def flat_bcast(row, n):
    return row.rearrange("(a n) -> a n", a=1).to_broadcast((P, n))


class Chip:

    def __init__(self, nc):
        self.nc = nc
        self.all = ExitStack()
        self.rows_loaded, self.loads = self.sem("rows_loaded"), 0

    def sem(self, name):
        return self.all.enter_context(self.nc.semaphore(name))

    def sb(self, ctx, name, shape, dt):
        return ctx.enter_context(self.nc.sbuf_tensor(name, shape, dt))

    def ps(self, ctx, name, shape, dt):
        return ctx.enter_context(self.nc.psum_tensor(name, shape, dt))


def make_constants(chip, ident_d, ident32, ident16):
    nc = chip.nc
    loaded, made = chip.sem("ident_loaded"), chip.sem("ident_made")
    with nc.Block() as block:
        @block.sync
        def _(sp):
            sp.dma_start(ident32[:], ident_d).then_inc(loaded, 16)

        @block.vector
        def _(dve):
            dve.wait_ge(loaded, 16)
            nc.vector.tensor_copy(ident16[:], ident32[:]).then_inc(made, 1)
            dve.wait_ge(made, 1)


def load_rows(chip, *pairs):
    nc = chip.nc
    with nc.Block() as block:
        @block.sync
        def _(sp):
            for dst, src in pairs:
                sp.dma_start(dst, src).then_inc(chip.rows_loaded, 16)
            chip.loads += len(pairs)
            sp.wait_ge(chip.rows_loaded, 16 * chip.loads)


def rsqrt_steps(nc, dve, done, root_ready, n, var, root, tmp, rstd):
    dve.wait_ge(root_ready, 1)
    nc.vector.reciprocal(tmp, root).then_inc(done, 1)
    dve.wait_ge(done, n + 1)
    nc.vector.tensor_tensor(tmp, tmp, var, ALU.mult).then_inc(done, 1)
    dve.wait_ge(done, n + 2)
    nc.vector.tensor_tensor(tmp, tmp, root, ALU.add).then_inc(done, 1)
    dve.wait_ge(done, n + 3)
    nc.vector.tensor_scalar(tmp, tmp, 0.5, None, ALU.mult).then_inc(done, 1)
    dve.wait_ge(done, n + 4)
    nc.vector.reciprocal(rstd, tmp).then_inc(done, 1)
    dve.wait_ge(done, n + 5)
    return n + 5


def normalise(chip, tag, x, xn):
    nc = chip.nc
    done, root_ready = chip.sem(f"{tag}_ln_steps"), chip.sem(f"{tag}_ln_root")
    var_ready = chip.sem(f"{tag}_ln_var")
    with ExitStack() as ctx:
        stats = chip.sb(ctx, f"{tag}_stats", [P, T, 2, nc.vector.BN_STATS_DIM], F32)
        aggr = chip.sb(ctx, f"{tag}_aggr", [P, T, nc.vector.BN_AGGR_DIM], F32)
        small = chip.sb(ctx, f"{tag}_small", [P, 4, T], F32)
        var, root, tmp, rstd = (small[:, k, :] for k in range(4))
        block = ctx.enter_context(nc.Block())

        @block.vector
        def _(dve):
            n = 0
            for t in range(T):
                for h in range(2):
                    nc.vector.bn_stats(stats[:, t, h, :], x[:, t, h * HALF:(h + 1) * HALF]).then_inc(done, 1)
            n += 2 * T
            dve.wait_ge(done, n)
            for t in range(T):
                nc.vector.bn_aggr(aggr[:, t, :], stats[:, t, :, :]).then_inc(done, 1)
            n += T
            dve.wait_ge(done, n)
            nc.vector.tensor_scalar(var, aggr[:, :, 1], LN_EPS, None, ALU.add).then_inc(var_ready, 1)
            dve.wait_ge(var_ready, 1)
            rsqrt_steps(nc, dve, done, root_ready, n, var, root, tmp, rstd)
            for t in range(T):
                last = nc.vector.tensor_scalar(xn[:, t, :], x[:, t, :], aggr[:, t, 0:1], rstd[:, t:t + 1],
                                               ALU.subtract, ALU.mult)
                last.then_inc(done, 1)
            dve.wait_ge(done, n + 5 + T)

        @block.scalar
        def _(act):
            act.wait_ge(var_ready, 1)
            nc.scalar.activation(root, var, ACT.Sqrt).then_inc(root_ready, 1)


def transpose_split(chip, tag, src_tile, xt_hi, xt_lo, ident32):
    nc = chip.nc
    turned, hi_ready, lo_ready = (chip.sem(f"{tag}_{s}") for s in ("turned", "hi", "lo"))
    with ExitStack() as ctx:
        banks = [chip.ps(ctx, f"{tag}_turn{n}", [P, 4, P], F32) for n in range(2)]
        block = ctx.enter_context(nc.Block())
        units = [(t, h) for t in range(T) for h in range(2)]

        @block.tensor
        def _(pe):
            for n, (t, h) in enumerate(units):
                if n >= 2:
                    pe.wait_ge(lo_ready, n - 1)
                for k in range(4):
                    last = nc.tensor.transpose(banks[n % 2][:, k, :], src_tile(t, 4 * h + k), ident32[:])
                last.then_inc(turned, 1)

        @block.scalar
        def _(act):
            for n, (t, h) in enumerate(units):
                act.wait_ge(turned, n + 1)
                nc.scalar.activation(xt_hi[:, 4 * h:4 * h + 4, t * P:(t + 1) * P], banks[n % 2][:], ACT.Copy,
                                     scale=X_SCALE).then_inc(hi_ready, 1)

        @block.vector
        def _(dve):
            for n, (t, h) in enumerate(units):
                dve.wait_ge(hi_ready, n + 1)
                for k in range(4 * h, 4 * h + 4):
                    last = nc.vector.scalar_tensor_tensor(
                        out=xt_lo[:, k, t * P:(t + 1) * P], in0=banks[n % 2][:, k - 4 * h, :], scalar=X_SCALE,
                        in1=xt_hi[:, k, t * P:(t + 1) * P], op0=ALU.mult, op1=ALU.subtract)
                last.then_inc(lo_ready, 1)
            dve.wait_ge(lo_ready, len(units))


def project(chip, tag, xt_hi, xt_lo, w_d, n_w, addend, out):
    nc = chip.nc
    w_loaded = [chip.sem(f"{tag}_w_loaded{h}") for h in range(2)]
    w_hi_ready, w_lo_ready = chip.sem(f"{tag}_w_hi"), chip.sem(f"{tag}_w_lo")
    summed, taken = chip.sem(f"{tag}_summed"), chip.sem(f"{tag}_taken")
    with ExitStack() as ctx:
        stage = [chip.sb(ctx, f"{tag}_w{h}", [P, KD, HALF], F32) for h in range(2)]
        w_hi = [chip.sb(ctx, f"{tag}_whi{h}", [P, KD, HALF], F16) for h in range(2)]
        w_lo = [chip.sb(ctx, f"{tag}_wlo{h}", [P, KD, HALF], F16) for h in range(2)]
        acc = [chip.ps(ctx, f"{tag}_acc{n}", [P, HALF], F32) for n in range(2 * T)]
        block = ctx.enter_context(nc.Block())
        panels = [(w, h) for w in range(n_w) for h in range(2)]

        @block.sync
        def _(sp):
            for n, (w, h) in enumerate(panels):
                if n >= 2:
                    sp.wait_ge(w_lo_ready, n - 1)
                src = w_d[w, :, h * HALF:(h + 1) * HALF].rearrange("(k p) n -> p k n", p=P)
                sp.dma_start(stage[n % 2][:], src).then_inc(w_loaded[n % 2], 16)

        @block.scalar
        def _(act):
            for n, (w, h) in enumerate(panels):
                act.wait_ge(w_loaded[n % 2], 16 * (n // 2 + 1))
                if n >= 2:
                    act.wait_ge(summed, T * (n - 1))
                nc.scalar.activation(w_hi[n % 2][:], stage[n % 2][:], ACT.Copy, scale=W_SCALE).then_inc(w_hi_ready, 1)

        @block.vector
        def _(dve):
            def split(n):
                dve.wait_ge(w_hi_ready, n + 1)
                nc.vector.scalar_tensor_tensor(out=w_lo[n % 2][:], in0=stage[n % 2][:], scalar=W_SCALE,
                                               in1=w_hi[n % 2][:], op0=ALU.mult,
                                               op1=ALU.subtract).then_inc(w_lo_ready, 1)

            split(0)
            for n, (w, h) in enumerate(panels):
                if n + 1 < len(panels):
                    split(n + 1)
                for t in range(T):
                    dve.wait_ge(summed, T * n + t + 1)
                    nc.vector.scalar_tensor_tensor(out=out(w, t, h), in0=acc[T * h + t][:], scalar=UNSCALE,
                                                   in1=addend(w, t, h), op0=ALU.mult,
                                                   op1=ALU.add).then_inc(taken, 1)
            dve.wait_ge(taken, T * len(panels))

        @block.tensor
        def _(pe):
            for n, (w, h) in enumerate(panels):
                pe.wait_ge(w_lo_ready, n + 1)
                for t in range(T):
                    if n >= 2:
                        pe.wait_ge(taken, T * (n - 2) + t + 1)
                    for k in range(KD):
                        tok = slice(t * P, (t + 1) * P)
                        for q, (a, b) in enumerate(((xt_hi, w_hi), (xt_hi, w_lo), (xt_lo, w_hi))):
                            last = nc.tensor.matmul(acc[T * h + t][:], a[:, k, tok], b[n % 2][:, k, :],
                                                    start=(k == 0 and q == 0), stop=(k == KD - 1 and q == 2))
                    last.then_inc(summed, 1)


def heads_of(ap):
    return ap.rearrange("p (h d) -> p h d", d=HD)


def per_head(ap):
    return ap.unsqueeze(2).to_broadcast((P, HEADS, HD))


def quantise_queries(chip, q, q_t, exp_scale, ident16):
    nc = chip.nc
    step, turned, q_t_ready = chip.sem("qq_steps"), chip.sem("qq_turned"), chip.sem("qq_t_ready")
    with ExitStack() as ctx:
        amax = chip.sb(ctx, "qq_amax", [P, T, HEADS], F32)
        scale = chip.sb(ctx, "qq_scale", [P, T, HEADS], F32)
        inv = chip.sb(ctx, "qq_inv", [P, T, HEADS], F32)
        twice = chip.sb(ctx, "qq_twice", [P, T, HEADS, 2, HD], F16)
        bank = [chip.ps(ctx, f"qq_turn{n}", [P, 8, P], F16) for n in range(2)]
        block = ctx.enter_context(nc.Block())
        units = [(t, g) for t in range(T) for g in range(2)]

        @block.vector
        def _(dve):
            nc.vector.tensor_scalar(q[:], q[:], HD ** -0.5, None, ALU.mult).then_inc(step, 1)
            dve.wait_ge(step, 1)
            nc.vector.tensor_reduce(amax[:], q[:].rearrange("p t (h d) -> p t h d", d=HD), AX.X, ALU.max,
                                    apply_absolute_value=True).then_inc(step, 1)
            dve.wait_ge(step, 2)
            nc.vector.tensor_scalar(scale[:], amax[:], 1.0 / LEVELS, 1e-8, ALU.mult, ALU.max).then_inc(step, 1)
            dve.wait_ge(step, 3)
            nc.vector.reciprocal(inv[:], scale[:]).then_inc(step, 1)
            nc.vector.tensor_scalar(exp_scale[:].rearrange("p h t -> p t h"), scale[:], 1.0 / K_SCALE, None,
                                    ALU.mult).then_inc(step, 1)
            dve.wait_ge(step, 5)
            for t in range(T):
                nc.vector.tensor_tensor(heads_of(q[:, t, :]), heads_of(q[:, t, :]), per_head(inv[:, t, :]),
                                        ALU.mult).then_inc(step, 1)
            dve.wait_ge(step, 5 + T)
            for t in range(T):
                for c in range(2):
                    nc.vector.tensor_scalar(twice[:, t, :, c, :], heads_of(q[:, t, :]), MAGIC, MAGIC,
                                            ALU.add, ALU.subtract).then_inc(step, 1)
            for n, (t, g) in enumerate(units):
                dve.wait_ge(turned, n + 1)
                nc.vector.tensor_copy(q_t[:, 8 * g:8 * g + 8, t * P:(t + 1) * P], bank[n % 2][:]).then_inc(q_t_ready, 1)
            dve.wait_ge(q_t_ready, len(units))

        @block.tensor
        def _(pe):
            pe.wait_ge(step, 5 + 3 * T)
            for n, (t, g) in enumerate(units):
                if n >= 2:
                    pe.wait_ge(q_t_ready, n - 1)
                for h in range(8):
                    last = nc.tensor.transpose(bank[n % 2][:, h, :],
                                               twice[:, t, 8 * g + h, :, :].rearrange("p c d -> p (c d)"), ident16[:])
                last.then_inc(turned, 1)


def keys_and_values(chip, ctx_d, wkv_d, bkv_d, kt_d, v_d, vmax, ident32, ident16):
    nc = chip.nc
    NC = 2 * D // HALF
    w_hi_ready, w_lo_ready = (chip.sem(f"kv_w_{s}") for s in ("hi", "lo"))
    w_loaded = [chip.sem(f"kv_w_loaded{h}") for h in range(2)]
    bias_loaded, vmax_cleared = chip.sem("kv_bias_loaded"), chip.sem("kv_vmax_cleared")
    with ExitStack() as ctx:
        w_hi = chip.sb(ctx, "kv_whi", [P, NC, KD, HALF], F16)
        w_lo = chip.sb(ctx, "kv_wlo", [P, NC, KD, HALF], F16)
        bias = chip.sb(ctx, "kv_bias", [P, 2 * D], F32)
        with ExitStack() as stage_ctx:
            stage = [chip.sb(stage_ctx, f"kv_stage{n}", [P, KD, HALF], F32) for n in range(2)]
            block = stage_ctx.enter_context(nc.Block())

            @block.sync
            def _(sp):
                sp.dma_start(bias[:], flat_bcast(bkv_d, 2 * D)).then_inc(bias_loaded, 16)
                for c in range(NC):
                    if c >= 2:
                        sp.wait_ge(w_lo_ready, c - 1)
                    sp.dma_start(stage[c % 2][:], wkv_d[:, c * HALF:(c + 1) * HALF].rearrange(
                        "(k p) n -> p k n", p=P)).then_inc(w_loaded[c % 2], 16)

            @block.scalar
            def _(act):
                for c in range(NC):
                    act.wait_ge(w_loaded[c % 2], 16 * (c // 2 + 1))
                    nc.scalar.activation(w_hi[:, c], stage[c % 2][:], ACT.Copy, scale=W_SCALE).then_inc(w_hi_ready, 1)

            @block.vector
            def _(dve):
                nc.vector.memset(vmax[:], 0.0).then_inc(vmax_cleared, 1)
                for c in range(NC):
                    dve.wait_ge(w_hi_ready, c + 1)
                    nc.vector.scalar_tensor_tensor(out=w_lo[:, c], in0=stage[c % 2][:], scalar=W_SCALE, in1=w_hi[:, c],
                                                   op0=ALU.mult, op1=ALU.subtract).then_inc(w_lo_ready, 1)
                dve.wait_ge(w_lo_ready, NC)

        rows = [chip.sb(ctx, f"kv_rows{s}", [P, D], F32) for s in range(2)]
        xt_hi = [chip.sb(ctx, f"kv_xthi{s}", [P, KD, P], F16) for s in range(2)]
        xt_lo = [chip.sb(ctx, f"kv_xtlo{s}", [P, KD, P], F16) for s in range(2)]
        key = [chip.sb(ctx, f"kv_key{s}", [P, D], F32) for s in range(2)]
        amax, scale, inv, scale64 = (chip.sb(ctx, f"kv_{n}", [P, HEADS], F32) for n in ("amax", "scale", "inv", "sc64"))
        parts = [chip.sb(ctx, f"kv_parts{s}", [P, HEADS, 2, HD], F16) for s in range(2)]
        kt = chip.sb(ctx, "kv_kt", [P, HEADS, 2 * P], F16)
        val = chip.sb(ctx, "kv_val", [P, HEADS, 2, HD], F32)
        vabs = chip.sb(ctx, "kv_vabs", [P, D], F32)
        acc = [chip.ps(ctx, f"kv_acc{c}", [P, HALF], F32) for c in range(NC)]
        turn = chip.ps(ctx, "kv_turn", [P, KD, P], F32)
        kturn = chip.ps(ctx, "kv_kturn", [P, HEADS, P], F16)
        rows_loaded = [chip.sem(f"kv_rows_loaded{s}") for s in range(2)]
        rows_turned = chip.sem("kv_rows_turned")
        hi_ready, lo_ready = chip.sem("kv_xt_hi"), chip.sem("kv_xt_lo")
        summed, taken = chip.sem("kv_summed"), chip.sem("kv_taken")
        step, int_ready = chip.sem("kv_steps"), chip.sem("kv_int_ready")
        khi_ready, parts_ready = chip.sem("kv_khi"), chip.sem("kv_parts_ready")
        keys_turned, kt_ready = chip.sem("kv_keys_turned"), chip.sem("kv_kt_ready")
        abs_ready = chip.sem("kv_abs")
        kt_stored, v_stored, v_ready = chip.sem("kv_kt_stored"), chip.sem("kv_v_stored"), chip.sem("kv_v_ready")
        block = ctx.enter_context(nc.Block())
        LAST_PAIR = KVT // 2 - 1
        STEPS = 6

        def each_pair(eng, body):
            body(0, True, False)
            with eng.Fori(1, LAST_PAIR) as i:
                body(i, False, False)
            body(LAST_PAIR, False, True)

        @block.sync
        def _(sp):
            def load(row, s):
                sp.dma_start(rows[s][:], row).then_inc(rows_loaded[s], 16)

            def store_keys(i):
                dst = kt_d[:, :, bass.ds(i * (2 * P), 2 * P)].rearrange("h p n -> p h n")
                sp.dma_start(dst, kt[:]).then_inc(kt_stored, 16)

            load(ctx_d[0], 0)
            load(ctx_d[1], 1)

            def body(i, first, last):
                if not first:
                    sp.wait_ge(kt_ready, 2 * i)
                    store_keys(i - 1)
                if not last:
                    for s in range(2):
                        sp.wait_ge(rows_turned, 2 * i + s + 1)
                        load(ctx_d[bass.ds(2 * i + 2 + s, 1)].rearrange("a p n -> (a p) n"), s)
                sp.wait_ge(v_ready, 2 * i + 2)
                dst = v_d[:, :, bass.ds(2 * i, 2), :].rearrange("h p a d -> p h a d")
                sp.dma_start(dst, val[:]).then_inc(v_stored, 16)

            each_pair(sp, body)
            sp.wait_ge(kt_ready, KVT)
            store_keys(LAST_PAIR)
            sp.wait_ge(kt_stored, 16 * (LAST_PAIR + 1))
            sp.wait_ge(v_stored, 16 * (LAST_PAIR + 1))

        @block.tensor
        def _(pe):
            def turn_rows(i, s):
                pe.wait_ge(rows_loaded[s], 16 * i + 16)
                for k in range(KD):
                    last = nc.tensor.transpose(turn[:, k, :], rows[s][:, k * P:(k + 1) * P], ident32[:])
                last.then_inc(rows_turned, 1)

            def turn_keys(u, s):
                pe.wait_ge(parts_ready, u + 1)
                for h in range(HEADS):
                    last = nc.tensor.transpose(kturn[:, h, :], parts[s][:, h].rearrange("p c d -> p (c d)"), ident16[:])
                last.then_inc(keys_turned, 1)

            def products(u, s, c):
                for k in range(KD):
                    for q, (a, b) in enumerate(((xt_hi, w_hi), (xt_hi, w_lo), (xt_lo, w_hi))):
                        last = nc.tensor.matmul(acc[c][:], a[s][:, k, :], b[:, c, k, :],
                                                start=(k == 0 and q == 0), stop=(k == KD - 1 and q == 2))
                last.then_inc(summed, 1)

            def body(i, first, last):
                for s in range(2):
                    u = 2 * i + s
                    pe.wait_ge(lo_ready, u + 1)
                    for c in range(NC):
                        if not (first and s == 0):
                            pe.wait_ge(taken, NC * (u - 1) + c + 1)
                        products(u, s, c)
                        if c == 0 and not (last and s == 1):
                            turn_rows(i + s, 1 - s)
                        if c == 1 and not (first and s == 0):
                            if not (first and s == 1):
                                pe.wait_ge(kt_ready, u - 1)
                            turn_keys(u - 1, 1 - s)

            turn_rows(0, 0)
            each_pair(pe, body)
            pe.wait_ge(kt_ready, KVT - 1)
            turn_keys(KVT - 1, 1)

        @block.scalar
        def _(act):
            def rows_high(u, s):
                act.wait_ge(rows_turned, u + 1)
                nc.scalar.activation(xt_hi[s][:], turn[:], ACT.Copy, scale=X_SCALE).then_inc(hi_ready, 1)

            def keys_out(u, s, wait_store, i):
                act.wait_ge(keys_turned, u + 1)
                if wait_store:
                    act.wait_ge(kt_stored, 16 * i)
                nc.scalar.activation(kt[:, :, s * P:(s + 1) * P], kturn[:], ACT.Copy).then_inc(kt_ready, 1)

            def body(i, first, last):
                for s in range(2):
                    u = 2 * i + s
                    if not (last and s == 1):
                        rows_high(u + 1, 1 - s)
                    if not (first and s == 0):
                        keys_out(u - 1, 1 - s, s == 1 and not first, i)
                    act.wait_ge(int_ready, u + 1)
                    nc.scalar.activation(parts[s][:, :, 0, :], heads_of(key[s][:]), ACT.Copy).then_inc(khi_ready, 1)
                    act.wait_ge(taken, NC * (u + 1))
                    if not (first and s == 0):
                        act.wait_ge(v_ready, u)
                    nc.scalar.activation(heads_of(vabs[:]), val[:, :, s, :], ACT.Abs).then_inc(abs_ready, 1)

            rows_high(0, 0)
            each_pair(act, body)
            keys_out(KVT - 1, 1, False, None)

        @block.vector
        def _(dve):
            def rows_low(u, s):
                dve.wait_ge(hi_ready, u + 1)
                nc.vector.scalar_tensor_tensor(out=xt_lo[s][:], in0=turn[:], scalar=X_SCALE, in1=xt_hi[s][:],
                                               op0=ALU.mult, op1=ALU.subtract).then_inc(lo_ready, 1)

            def key_chunk(u, s, c):
                dve.wait_ge(summed, NC * u + c + 1)
                cols = slice(c * HALF, (c + 1) * HALF)
                nc.vector.scalar_tensor_tensor(out=key[s][:, cols], in0=acc[c][:], scalar=UNSCALE,
                                               in1=bias[:, cols], op0=ALU.mult, op1=ALU.add).then_inc(taken, 1)

            def quantise(u, s):
                n = STEPS * u
                dve.wait_ge(taken, NC * u + 2)
                nc.vector.tensor_reduce(amax[:], heads_of(key[s][:]), AX.X, ALU.max,
                                        apply_absolute_value=True).then_inc(step, 1)
                dve.wait_ge(step, n + 1)
                nc.vector.tensor_scalar(scale[:], amax[:], 1.0 / LEVELS, 1e-8, ALU.mult, ALU.max).then_inc(step, 1)
                dve.wait_ge(step, n + 2)
                nc.vector.reciprocal(inv[:], scale[:]).then_inc(step, 1)
                nc.vector.tensor_scalar(scale64[:], scale[:], K_SCALE, None, ALU.mult).then_inc(step, 1)
                dve.wait_ge(step, n + 4)
                nc.vector.tensor_tensor(heads_of(key[s][:]), heads_of(key[s][:]), per_head(inv[:]),
                                        ALU.mult).then_inc(step, 1)
                dve.wait_ge(step, n + 5)
                nc.vector.tensor_scalar(key[s][:], key[s][:], MAGIC, MAGIC, ALU.add, ALU.subtract).then_inc(step, 1)
                dve.wait_ge(step, n + 6)
                nc.vector.tensor_tensor(heads_of(key[s][:]), heads_of(key[s][:]), per_head(scale64[:]),
                                        ALU.mult).then_inc(int_ready, 1)

            def low_parts(u, s):
                dve.wait_ge(khi_ready, u + 1)
                nc.vector.tensor_tensor(parts[s][:, :, 1, :], heads_of(key[s][:]), parts[s][:, :, 0, :],
                                        ALU.subtract).then_inc(parts_ready, 1)

            def value_chunk(u, s, c):
                dve.wait_ge(summed, NC * u + c + 1)
                cols = slice(c * HALF, (c + 1) * HALF)
                h = (c - 2) * (HALF // HD)
                nc.vector.scalar_tensor_tensor(
                    out=val[:, h:h + HALF // HD, s, :], in0=acc[c][:].rearrange("p (h d) -> p h d", d=HD),
                    scalar=UNSCALE, in1=bias[:, cols].rearrange("p (h d) -> p h d", d=HD),
                    op0=ALU.mult, op1=ALU.add).then_inc(taken, 1)

            def value_max(u, s, start):
                if not start:
                    dve.wait_ge(v_ready, u)
                dve.wait_ge(abs_ready, u + 1)
                nc.vector.tensor_tensor(vmax[:], vabs[:], vmax[:], ALU.max).then_inc(v_ready, 1)

            def body(i, first, last):
                for s in range(2):
                    u = 2 * i + s
                    key_chunk(u, s, 0)
                    if not (last and s == 1):
                        rows_low(u + 1, 1 - s)
                    key_chunk(u, s, 1)
                    quantise(u, s)
                    if s == 0 and not first:
                        dve.wait_ge(v_stored, 16 * i)
                    value_chunk(u, s, 2)
                    low_parts(u, s)
                    value_chunk(u, s, 3)
                    value_max(u, s, first and s == 0)

            dve.wait_ge(bias_loaded, 16)
            rows_low(0, 0)
            each_pair(dve, body)
            dve.wait_ge(v_ready, KVT)


def value_scales(chip, vmax, scale_d, v_scale, v_inv, ident32):
    nc = chip.nc
    turned, reduced, out, back, step = (chip.sem(f"vs_{n}") for n in ("turned", "reduced", "out", "back", "steps"))
    with ExitStack() as ctx:
        col = chip.sb(ctx, "vs_col", [P, KD], F32)
        bank = chip.ps(ctx, "vs_turn", [P, KD, P], F32)
        block = ctx.enter_context(nc.Block())

        @block.tensor
        def _(pe):
            for k in range(KD):
                last = nc.tensor.transpose(bank[:, k, :], vmax[:, k * P:(k + 1) * P], ident32[:])
            last.then_inc(turned, 1)

        @block.vector
        def _(dve):
            dve.wait_ge(turned, 1)
            nc.vector.tensor_reduce(col[:], bank[:], AX.X, ALU.max).then_inc(step, 1)
            dve.wait_ge(step, 1)
            nc.vector.tensor_scalar(col[:], col[:], 1.0 / LEVELS, 1e-8, ALU.mult, ALU.max).then_inc(reduced, 1)
            dve.wait_ge(back, 16)
            nc.vector.reciprocal(v_inv[:], v_scale[:]).then_inc(step, 1)
            dve.wait_ge(step, 2)

        @block.sync
        def _(sp):
            sp.wait_ge(reduced, 1)
            sp.dma_start(scale_d.rearrange("(k p) -> p k", p=P), col[:], allow_slow_non_contiguous=True).then_inc(out, 16)
            sp.wait_ge(out, 16)
            sp.dma_start(v_scale[:], flat_bcast(scale_d, D)).then_inc(back, 16)
            sp.wait_ge(back, 16)


def attend_quantised(chip, q_t, exp_scale, kt_d, v_d, v_scale, v_inv, o, ident16):
    nc = chip.nc
    SLOTS = 2 * T
    SC = 1024
    CH = NKV // SC
    GB = SC // P
    EC = 2048
    NE = NKV // EC
    PAIRS = HEADS // 2
    AHEAD = 2
    LN_TOP = float(np.log(255.0))
    kt_loaded = [chip.sem(f"at_kt_loaded{j}") for j in range(2)]
    v_loaded, q_ready, v_quantised = chip.sem("at_v_loaded"), chip.sem("at_q_ready"), chip.sem("at_v_quant")
    v_step, filled, copied = chip.sem("at_v_steps"), chip.sem("at_filled"), chip.sem("at_copied")
    bias_ready, bias_step, exp_done = chip.sem("at_bias_ready"), chip.sem("at_bias_steps"), chip.sem("at_exp")
    turned, summed = chip.sem("at_turned"), chip.sem("at_summed")
    magic_set = chip.sem("at_magic_set")
    out_even, out_odd = chip.sem("at_out_even"), chip.sem("at_out_odd")
    inv_step, o_taken, o_moved = chip.sem("at_inv_steps"), chip.sem("at_o_taken"), chip.sem("at_o_moved")
    COPIED0, EXP0, TURNED0, BANK0, SUMMED0, TAKEN0, MOVED0 = 2, 2 * NE, 4, 1, 4, 2, 2
    with ExitStack() as ctx:
        kt = [chip.sb(ctx, f"at_kt{j}", [P, NKV], F16) for j in range(2)]
        magic = chip.sb(ctx, "at_magic", [P, 1], F32)
        v_raw = chip.sb(ctx, "at_v_raw", [P, KVT, HD], F32)
        v_int = [chip.sb(ctx, f"at_v_int{j}", [P, KVT, HD], F16) for j in range(2)]
        sc = [chip.sb(ctx, f"at_sc{j}", [P, NKV], F32) for j in range(2)]
        prob = [chip.sb(ctx, f"at_prob{j}", [P, EC], U16) for j in range(2)]
        probt = [chip.sb(ctx, f"at_probt{j}", [P, GB, P], F16) for j in range(4)]
        q_pair = [chip.sb(ctx, f"at_q{j}", [P, T * P], F16) for j in range(2)]
        qs_pair = [chip.sb(ctx, f"at_qs{j}", [P, T], F32) for j in range(2)]
        vs_pair = [chip.sb(ctx, f"at_vs{j}", [P, HD], F32) for j in range(2)]
        vi_head = chip.sb(ctx, "at_vi", [P, HD], F32)
        o_pair = [chip.sb(ctx, f"at_o{j}", [P, T, HD], F32) for j in range(2)]
        part_max = [chip.sb(ctx, f"at_pmax{j}", [P, CH], F32) for j in range(2)]
        neg_max = [chip.sb(ctx, f"at_nmax{j}", [P, 1], F32) for j in range(2)]
        bias = [chip.sb(ctx, f"at_bias{j}", [P, 1], F32) for j in range(2)]
        part_sum = [chip.sb(ctx, f"at_psum{j}", [P, NE], F32) for j in range(2)]
        total = [chip.sb(ctx, f"at_total{j}", [P, 1], F32) for j in range(2)]
        inv = [chip.sb(ctx, f"at_inv{j}", [P, 1], F32) for j in range(2)]
        score = [chip.ps(ctx, f"at_score{j}", [P, SC], F32) for j in range(2)]
        turn = [chip.ps(ctx, f"at_turn{j}", [P, GB, P], F16) for j in range(2)]
        outp = [chip.ps(ctx, f"at_outp{j}", [P, HALF], F32) for j in range(2)]
        block = ctx.enter_context(nc.Block())

        def each_pair(eng, body):
            with eng.Fori(0, PAIRS - 1) as i:
                body(i, False)
            body(PAIRS - 1, True)

        @block.sync
        def _(sp):
            def load(head, j, before_v):
                sp.dma_start(kt[j][:], kt_d[bass.ds(head, 1)].rearrange("a p n -> (a p) n")).then_inc(kt_loaded[j], 16)
                if before_v is not None:
                    sp.wait_ge(v_quantised, before_v)
                sp.dma_start(v_raw[:], v_d[bass.ds(head, 1)].rearrange("a p n d -> (a p) n d")).then_inc(v_loaded, 16)

            load(0, 0, None)
            load(1, 1, 1)
            with sp.Fori(0, PAIRS - 1) as i:
                for j in range(2):
                    sp.wait_ge(filled, CH * (i * SLOTS + T * (j + 1)))
                    load(2 * i + 2 + j, j, 2 * i + 2 + j)
            sp.wait_ge(v_loaded, 16 * HEADS)

        @block.gpsimd
        def _(pool):
            pool.sem_inc(o_moved, MOVED0)
            rounder = magic[:].unsqueeze(2).to_broadcast((P, KVT, HD))
            nc.gpsimd.memset(magic[:], MAGIC).then_inc(magic_set, 1)
            pool.wait_ge(magic_set, 1)

            def fetch(head, j):
                nc.gpsimd.tensor_copy(q_pair[j][:], q_t[:, bass.ds(head, 1), :].rearrange("p a n -> p (a n)"))\
                    .then_inc(q_ready, 1)
                nc.gpsimd.tensor_copy(qs_pair[j][:], exp_scale[:, bass.ds(head, 1), :].rearrange("p a n -> p (a n)"))\
                    .then_inc(q_ready, 1)
                nc.gpsimd.tensor_copy(vs_pair[j][:], v_scale[:, bass.ds(head * HD, HD)]).then_inc(v_step, 1)
                nc.gpsimd.tensor_copy(vi_head[:], v_inv[:, bass.ds(head * HD, HD)]).then_inc(v_step, 1)
                pool.wait_ge(v_step, 4 * head + 2)
                pool.wait_ge(v_loaded, 16 * head + 16)
                nc.gpsimd.tensor_tensor(v_raw[:], v_raw[:], vi_head[:].unsqueeze(1).to_broadcast((P, KVT, HD)),
                                        ALU.mult).then_inc(v_step, 1)
                pool.wait_ge(v_step, 4 * head + 3)
                nc.gpsimd.tensor_tensor(v_raw[:], v_raw[:], rounder, ALU.add).then_inc(v_step, 1)
                pool.wait_ge(v_step, 4 * head + 4)
                nc.gpsimd.tensor_tensor(v_int[j][:], v_raw[:], rounder, ALU.subtract).then_inc(v_quantised, 1)

            def move_out(i, j):
                head = 2 * i + j
                pool.wait_ge(o_taken, TAKEN0 + i * SLOTS + T * (j + 1))
                nc.gpsimd.tensor_copy(o[:, :, bass.ds(head * HD, HD)], o_pair[j][:]).then_inc(o_moved, 1)

            fetch(0, 0)
            fetch(1, 1)

            def body(i, last):
                for j in range(2):
                    move_out(i, j)
                    if not last:
                        fetch(2 * i + 2 + j, j)

            each_pair(pool, body)
            pool.wait_ge(o_moved, MOVED0 + HEADS)

        @block.tensor
        def _(pe):
            pe.sem_inc(turned, TURNED0)
            pe.sem_inc(summed, SUMMED0)

            def scores(g, n, c):
                n = n % SLOTS
                j, t = n // T, n % T
                pe.wait_ge(copied, g * CH + c - 1 + COPIED0)
                for b in range(SC // HALF):
                    cols = slice(c * SC + b * HALF, c * SC + (b + 1) * HALF)
                    last = nc.tensor.matmul(score[c % 2][:, b * HALF:(b + 1) * HALF], q_pair[j][:, t * P:(t + 1) * P],
                                            kt[j][:, cols], start=True, stop=True)
                last.then_inc(filled, 1)

            def turns(g, c):
                if c % 2 == 0:
                    pe.wait_ge(exp_done, EXP0 + g * NE + c // 2 + 1)
                    pe.wait_ge(out_even, BANK0 + g * (CH // 2) + c // 2)
                else:
                    pe.wait_ge(out_odd, BANK0 + g * (CH // 2) + c // 2)
                for b in range(GB):
                    at = (c % 2) * SC + b * P
                    last = nc.tensor.transpose(turn[c % 2][:, b, :], prob[(c // 2) % 2][:, at:at + P].bitcast(F16),
                                               ident16[:])
                last.then_inc(turned, 1)

            def sums(g, n, c):
                if c == 0:
                    pe.wait_ge(o_taken, g + 1 - 2 + TAKEN0)
                pe.wait_ge((out_even, out_odd)[c % 2], BANK0 + g * (CH // 2) + c // 2 + 1)
                for b in range(GB):
                    last = nc.tensor.matmul(outp[n % 2][:, 0:HD], probt[c % 4][:, b, :], v_int[n // T][:, c * GB + b, :],
                                            start=(c == 0 and b == 0), stop=(c == CH - 1 and b == GB - 1))
                last.then_inc(summed, 1)

            def inputs_ready(i, n):
                if n % T == 0:
                    k, j = n // SLOTS, (n % SLOTS) // T
                    pe.wait_ge(kt_loaded[j], (i + k) * 16 + 16)
                    pe.wait_ge(q_ready, 4 * (i + k) + 2 * j + 2)

            def body(i, last):
                for n in range(SLOTS):
                    g = i * SLOTS + n
                    for c in range(CH):
                        ahead, cc = (n + 1, c + AHEAD) if c + AHEAD < CH else (n + 2, c + AHEAD - CH)
                        if not (last and ahead >= SLOTS):
                            if cc == 0:
                                inputs_ready(i, ahead)
                            scores(i * SLOTS + ahead, ahead, cc)
                        if c % 2 == 1:
                            turns(g, c - 1)
                            turns(g, c)
                            if c >= 3:
                                if c == 3 and n % T == 0:
                                    pe.wait_ge(v_quantised, 2 * i + n // T + 1)
                                sums(g, n, c - 3)
                                sums(g, n, c - 2)
                    sums(g, n, CH - 2)
                    sums(g, n, CH - 1)

            inputs_ready(0, 0)
            for c in range(CH + AHEAD):
                scores(c // CH, c // CH, c % CH)
            each_pair(pe, body)

        @block.vector
        def _(dve):
            dve.sem_inc(copied, COPIED0)
            dve.sem_inc(out_even, BANK0)
            dve.sem_inc(o_taken, TAKEN0)

            def copy(g, n, c):
                if c == 0:
                    dve.wait_ge(exp_done, (g - 1) * NE + EXP0)
                dve.wait_ge(filled, g * CH + c + 1)
                nc.vector.tensor_scalar(sc[n % 2][:, c * SC:(c + 1) * SC], score[c % 2][:], 1.0, None, ALU.mult, ALU.max,
                                        accum_out=part_max[n % 2][:, c:c + 1]).then_inc(copied, 1)

            def make_bias(g, n):
                dve.wait_ge(copied, COPIED0 + (g + 1) * CH)
                nc.vector.tensor_reduce(neg_max[n % 2][:], part_max[n % 2][:], AX.X, ALU.max, negate=True)\
                    .then_inc(bias_step, 1)
                dve.wait_ge(bias_step, g + 1)
                j, t = (n % SLOTS) // T, n % T
                nc.vector.tensor_scalar(bias[n % 2][:], neg_max[n % 2][:], qs_pair[j][:, t:t + 1], LN_TOP,
                                        ALU.mult, ALU.add).then_inc(bias_ready, 1)

            def turned_out(g, c):
                dve.wait_ge(turned, TURNED0 + g * CH + c + 1)
                dve.wait_ge(summed, g * CH + c + 1 - 4 + SUMMED0)
                nc.vector.tensor_copy(probt[c % 4][:], turn[c % 2][:].bitcast(U16)).then_inc(out_even, 1)

            def output(i, g, n):
                dve.wait_ge(summed, SUMMED0 + (g + 1) * CH)
                nc.vector.tensor_reduce(total[n % 2][:], part_sum[n % 2][:], AX.X, ALU.add).then_inc(inv_step, 1)
                dve.wait_ge(inv_step, 2 * g + 1)
                nc.vector.reciprocal(inv[n % 2][:], total[n % 2][:]).then_inc(inv_step, 1)
                dve.wait_ge(inv_step, 2 * g + 2)
                j, t = n // T, n % T
                if t == 0:
                    dve.wait_ge(o_moved, 2 * i + j + 1 - 2 + MOVED0)
                nc.vector.scalar_tensor_tensor(out=o_pair[j][:, t, :], in0=outp[n % 2][:, 0:HD], scalar=inv[n % 2][:],
                                               in1=vs_pair[j][:], op0=ALU.mult, op1=ALU.mult).then_inc(o_taken, 1)

            def body(i, last):
                for n in range(SLOTS):
                    g = i * SLOTS + n
                    for c in range(CH):
                        ahead, cc = (n + 1, c + AHEAD) if c + AHEAD < CH else (n + 2, c + AHEAD - CH)
                        if not (last and ahead >= SLOTS):
                            copy(i * SLOTS + ahead, ahead, cc)
                            if cc == CH - 1:
                                make_bias(i * SLOTS + ahead, ahead)
                        if c % 2 == 1:
                            turned_out(g, c - 1)
                    output(i, g, n)

            for c in range(CH + AHEAD):
                copy(c // CH, c // CH, c % CH)
                if c == CH - 1:
                    dve.wait_ge(q_ready, 2)
                    make_bias(0, 0)
            each_pair(dve, body)
            dve.wait_ge(o_taken, TAKEN0 + HEADS * T)

        @block.scalar
        def _(act):
            act.sem_inc(exp_done, EXP0)
            act.sem_inc(out_odd, BANK0)

            def exps(g, n, e):
                if e == 0:
                    act.wait_ge(bias_ready, g + 1)
                    act.wait_ge(o_taken, g + 1 - 2 + TAKEN0)
                act.wait_ge(turned, (g * NE + e - 2) * 2 + 2 + TURNED0)
                j, t = n // T, n % T
                nc.scalar.activation(prob[e % 2][:], sc[n % 2][:, e * EC:(e + 1) * EC], ACT.Exp, bias=bias[n % 2][:],
                                     scale=qs_pair[j][:, t:t + 1], accum_out=part_sum[n % 2][:, e:e + 1])\
                    .then_inc(exp_done, 1)

            def turned_out(g, c):
                act.wait_ge(turned, TURNED0 + g * CH + c + 1)
                act.wait_ge(summed, g * CH + c + 1 - 4 + SUMMED0)
                nc.scalar.activation(probt[c % 4][:], turn[c % 2][:].bitcast(U16), ACT.Copy).then_inc(out_odd, 1)

            def body(i, last):
                for n in range(SLOTS):
                    g = i * SLOTS + n
                    exps(g, n, 0)
                    for e in range(1, NE):
                        exps(g, n, e)
                        turned_out(g, 2 * e - 1)
                    turned_out(g, CH - 1)

            each_pair(act, body)
            act.wait_ge(out_odd, BANK0 + HEADS * T * CH // 2)


def rotate(chip, y_q, y_k, cos, sin):
    nc = chip.nc
    q_step, k_step = chip.sem("rope_q_steps"), chip.sem("rope_k_steps")
    with ExitStack() as ctx:
        swapped = [chip.sb(ctx, f"rope_sw{j}", [P, T * HEADS, HD], F32) for j in range(2)]
        block = ctx.enter_context(nc.Block())

        def turn_pairs(wait, engine, y, step, sw):
            rows = y[:].rearrange("p t (h d) -> p (t h) d", d=HD)
            pairs, out = (a.rearrange("p r (i e) -> p r i e", e=2) for a in (rows, sw[:]))
            table = sin[:].rearrange("p (i e) -> p i e", e=2)
            for e in range(2):
                engine.tensor_tensor(out[:, :, :, e], pairs[:, :, :, 1 - e],
                                     table[:, :, e].unsqueeze(1).to_broadcast((P, T * HEADS, HD // 2)),
                                     ALU.mult).then_inc(step, 1)
            wait(step, 2)
            engine.tensor_tensor(rows, rows, cos[:].unsqueeze(1).to_broadcast((P, T * HEADS, HD)),
                                 ALU.mult).then_inc(step, 1)
            wait(step, 3)
            engine.tensor_tensor(rows, rows, sw[:], ALU.add).then_inc(step, 1)
            wait(step, 4)

        @block.vector
        def _(dve):
            turn_pairs(dve.wait_ge, nc.vector, y_q, q_step, swapped[0])

        @block.gpsimd
        def _(pool):
            turn_pairs(pool.wait_ge, nc.gpsimd, y_k, k_step, swapped[1])


def attend_causal(chip, y_q, y_k, y_v, mask, o, ident32):
    nc = chip.nc
    turned, q_out, k_out = chip.sem("ca_turned"), chip.sem("ca_q_out"), chip.sem("ca_k_out")
    scored, masked, maxed = chip.sem("ca_scored"), chip.sem("ca_masked"), chip.sem("ca_maxed")
    exps_done, p_turned, p_out = chip.sem("ca_exp"), chip.sem("ca_p_turned"), chip.sem("ca_p_out")
    summed, inv_ready, o_ready = chip.sem("ca_summed"), chip.sem("ca_inv"), chip.sem("ca_o")
    HG = 4
    groups = [(t, c) for t in range(T) for c in range(HEADS // HG)]
    G = len(groups)

    def head_of(c, j):
        return 2 * HG * (c // 2) + 2 * j + c % 2

    with ExitStack() as ctx:
        q_t = chip.sb(ctx, "ca_qt", [P, KD, T * P], F32)
        k_t = chip.sb(ctx, "ca_kt", [P, KD, T * P], F32)
        s = [chip.sb(ctx, f"ca_s{j}", [P, HG, P], F32) for j in range(2)]
        p_t = [chip.sb(ctx, f"ca_pt{j}", [P, HG, P], F32) for j in range(2)]
        neg_max = [chip.sb(ctx, f"ca_nm{j}", [P, HG], F32) for j in range(2)]
        total = [chip.sb(ctx, f"ca_tot{j}", [P, HG], F32) for j in range(2)]
        inv = [chip.sb(ctx, f"ca_inv{j}", [P, HG], F32) for j in range(2)]
        with ExitStack() as tctx:
            bq = [chip.ps(tctx, f"ca_bq{n}", [P, 4, P], F32) for n in range(2)]
            bk = [chip.ps(tctx, f"ca_bk{n}", [P, 4, P], F32) for n in range(2)]
            block = tctx.enter_context(nc.Block())
            units = [(t, h) for t in range(T) for h in range(2)]

            @block.tensor
            def _(pe):
                for n, (t, h) in enumerate(units):
                    if n >= 2:
                        pe.wait_ge(q_out, n - 1)
                        pe.wait_ge(k_out, n - 1)
                    for y, bank in ((y_q, bq), (y_k, bk)):
                        for k in range(4):
                            at = (4 * h + k) * P
                            last = nc.tensor.transpose(bank[n % 2][:, k, :], y[:, t, at:at + P], ident32[:])
                    last.then_inc(turned, 1)

            @block.scalar
            def _(act):
                for n, (t, h) in enumerate(units):
                    act.wait_ge(turned, n + 1)
                    nc.scalar.activation(q_t[:, 4 * h:4 * h + 4, t * P:(t + 1) * P], bq[n % 2][:], ACT.Copy)\
                        .then_inc(q_out, 1)

            @block.vector
            def _(dve):
                for n, (t, h) in enumerate(units):
                    dve.wait_ge(turned, n + 1)
                    nc.vector.tensor_copy(k_t[:, 4 * h:4 * h + 4, t * P:(t + 1) * P], bk[n % 2][:])\
                        .then_inc(k_out, 1)
                dve.wait_ge(k_out, len(units))

        score = [chip.ps(ctx, f"ca_score{n}", [P, HG, P], F32) for n in range(2)]
        turn = [chip.ps(ctx, f"ca_turn{n}", [P, HG, P], F32) for n in range(2)]
        outp = [chip.ps(ctx, f"ca_outp{n}", [P, HG, P], F32) for n in range(2)]
        block = ctx.enter_context(nc.Block())

        @block.tensor
        def _(pe):
            def scores(g):
                t, c = groups[g]
                if g >= 2:
                    pe.wait_ge(masked, g - 1)
                for j in range(HG):
                    h = head_of(c, j)
                    rows, tok = slice(HD * (h % 2), HD * (h % 2) + HD), slice(t * P, (t + 1) * P)
                    last = nc.tensor.matmul(score[g % 2][:, j, :], q_t[rows, h // 2, tok], k_t[rows, h // 2, tok],
                                            start=True, stop=True)
                last.then_inc(scored, 1)

            def turns(g):
                pe.wait_ge(exps_done, HG * (g + 1))
                if g >= 2:
                    pe.wait_ge(p_out, g - 1)
                for j in range(HG):
                    last = nc.tensor.transpose(turn[g % 2][:, j, :], s[g % 2][:, j, :], ident32[:])
                last.then_inc(p_turned, 1)

            def sums(g):
                t, c = groups[g]
                pe.wait_ge(p_out, g + 1)
                if g >= 2:
                    pe.wait_ge(o_ready, g - 1)
                for j in range(HG):
                    h = head_of(c, j)
                    last = nc.tensor.matmul(outp[g % 2][:, j, 0:HD], p_t[g % 2][:, j, :], y_v[:, t, h * HD:(h + 1) * HD],
                                            start=True, stop=True)
                last.then_inc(summed, 1)

            scores(0)
            for g in range(G):
                if g + 1 < G:
                    scores(g + 1)
                turns(g)
                if g >= 1:
                    sums(g - 1)
            sums(G - 1)

        @block.vector
        def _(dve):
            def masks(g):
                dve.wait_ge(scored, g + 1)
                if g >= 2:
                    dve.wait_ge(p_turned, g - 1)
                nc.vector.scalar_tensor_tensor(out=s[g % 2][:], in0=score[g % 2][:], scalar=HD ** -0.5,
                                               in1=mask[:].unsqueeze(1).to_broadcast((P, HG, P)), op0=ALU.mult,
                                               op1=ALU.add).then_inc(masked, 1)
                dve.wait_ge(masked, g + 1)
                nc.vector.tensor_reduce(neg_max[g % 2][:], s[g % 2][:], AX.X, ALU.max, negate=True).then_inc(maxed, 1)

            def outputs(g):
                t, c = groups[g]
                dve.wait_ge(summed, g + 1)
                nc.vector.reciprocal(inv[g % 2][:], total[g % 2][:]).then_inc(inv_ready, 1)
                dve.wait_ge(inv_ready, g + 1)
                nc.vector.tensor_tensor(
                    o[:, t, :].rearrange("p (c h e d) -> p c h e d", h=HG, e=2, d=HD)[:, c // 2, :, c % 2, :],
                    outp[g % 2][:, :, 0:HD], inv[g % 2][:].unsqueeze(2).to_broadcast((P, HG, HD)),
                    ALU.mult).then_inc(o_ready, 1)

            masks(0)
            for g in range(G):
                if g + 1 < G:
                    masks(g + 1)
                if g >= 1:
                    outputs(g - 1)
            outputs(G - 1)
            dve.wait_ge(o_ready, G)

        @block.scalar
        def _(act):
            for g in range(G):
                act.wait_ge(maxed, g + 1)
                if g >= 2:
                    act.wait_ge(inv_ready, g - 1)
                for j in range(HG):
                    nc.scalar.activation(s[g % 2][:, j, :], s[g % 2][:, j, :], ACT.Exp, bias=neg_max[g % 2][:, j:j + 1],
                                         accum_out=total[g % 2][:, j:j + 1]).then_inc(exps_done, 1)
                act.wait_ge(p_turned, g + 1)
                if g >= 2:
                    act.wait_ge(summed, g - 1)
                nc.scalar.activation(p_t[g % 2][:], turn[g % 2][:], ACT.Copy).then_inc(p_out, 1)


def add_rows(chip, tag, out, a, row):
    nc = chip.nc
    done = chip.sem(f"{tag}_done")
    with nc.Block() as block:
        @block.vector
        def _(dve):
            nc.vector.tensor_tensor(out[:], a[:], row[:].unsqueeze(1).to_broadcast((P, T, D)), ALU.add).then_inc(done, 1)
            dve.wait_ge(done, 1)


MAGNITUDE, SIGN = 0x0E000E00, 0x80008000 - (1 << 32)


def shift_of(bits):
    return (ALU.logical_shift_left, bits) if bits >= 0 else (ALU.logical_shift_right, -bits)


class Unpacker:

    def __init__(self, chip, ctx, tag, cols):
        self.nc, self.cols = chip.nc, cols
        self.mag = chip.sb(ctx, f"{tag}_mag", [P, 4, cols], I32)
        self.sign = chip.sb(ctx, f"{tag}_sign", [P, 4, cols], I32)
        self.prod = [chip.sb(ctx, f"{tag}_prod{j}", [P, 4, cols, 2], F32) for j in range(2)]
        self.step, self.taken = chip.sem(f"{tag}_steps"), chip.sem(f"{tag}_taken")
        self.prod_ready = chip.sem(f"{tag}_prod_ready")
        self.hi_ready, self.lo_ready = chip.sem(f"{tag}_hi"), chip.sem(f"{tag}_lo")

    LO0 = 2

    def product(self, dve, unit, j, packed, scale):
        nc = self.nc
        if unit:
            dve.wait_ge(self.prod_ready, unit)
        for k in range(4):
            op, by = shift_of(9 - 4 * k)
            nc.vector.tensor_scalar(self.mag[:, k, :], packed, by, MAGNITUDE, op, ALU.bitwise_and).then_inc(self.step, 1)
            op, by = shift_of(12 - 4 * k)
            nc.vector.tensor_scalar(self.sign[:, k, :], packed, by, SIGN, op, ALU.bitwise_and)\
                .then_inc(self.taken if k == 3 else self.step, 1)
        dve.wait_ge(self.step, 8 * unit + 7)
        dve.wait_ge(self.taken, unit + 1)
        nc.vector.tensor_tensor(self.mag[:], self.mag[:], self.sign[:], ALU.bitwise_or).then_inc(self.step, 1)
        dve.wait_ge(self.step, 8 * unit + 8)
        dve.wait_ge(self.lo_ready, unit - 1 + self.LO0)
        codes = self.mag[:].bitcast(F16).rearrange("p k (n e) -> p k n e", e=2)
        nc.vector.tensor_tensor(self.prod[j][:], codes, scale.unsqueeze(1).unsqueeze(3).to_broadcast(
            (P, 4, self.cols, 2)), ALU.mult).then_inc(self.prod_ready, 1)

    @staticmethod
    def by_word(ap):
        return ap.rearrange("p (e k) n -> p k n e", e=2)

    def high(self, act, unit, j, dst):
        act.wait_ge(self.prod_ready, unit + 1)
        for k in range(4):
            last = self.nc.scalar.activation(self.by_word(dst)[:, k], self.prod[j][:, k], ACT.Copy)
        last.then_inc(self.hi_ready, 1)

    def low(self, pool, unit, j, dst_hi, dst):
        pool.wait_ge(self.hi_ready, unit + 1)
        self.nc.gpsimd.tensor_tensor(self.by_word(dst), self.prod[j][:], self.by_word(dst_hi),
                                     ALU.subtract).then_inc(self.lo_ready, 1)


def feed_forward(chip, xt_hi, xt_lo, gu_d, gu_scale_d, dn_d, dn_scale_d, x, spare, out_d, ident32):
    nc = chip.nc
    QC = 2
    NQ = WORD // QC
    COLS = QC * P
    UP_OUT = 1.0 / (X_SCALE * SC_SCALE * NIB_SCALE)
    DOWN_OUT = 1.0 / (H_SCALE * SC_SCALE * NIB_SCALE)
    with ExitStack() as ctx:
        w_hi = [chip.sb(ctx, f"ff_whi{j}", [P, WORD, 2 * COLS], F16) for j in range(2)]
        w_lo = [chip.sb(ctx, f"ff_wlo{j}", [P, WORD, 2 * COLS], F16) for j in range(2)]
        h_hi = chip.sb(ctx, "ff_hhi", [P, NB * WORD, T * P], F16)
        h_lo = chip.sb(ctx, "ff_hlo", [P, NB * WORD, T * P], F16)
        dn_scale = chip.sb(ctx, "ff_dn_scale", [P, NB, D], F16)
        dn_rows = chip.sb(ctx, "ff_dn_rows", [P, D // P, NB * P], I32)
        dn_cleared, dn_loaded, dn_scaled = chip.sem("ff_dn_cleared"), chip.sem("ff_dn_loaded"), chip.sem("ff_dn_scaled")
        with ExitStack() as up:
            rows = [chip.sb(up, f"ff_rows{g}", [P, WORD, P], I32) for g in range(2)]
            raw = spare[:].rearrange("p t n -> p (t n)").bitcast(F16)[:, 0:2 * INNER]
            scale = chip.sb(up, "ff_scale", [P, 2 * NB, WORD, P], F16)
            sig = [chip.sb(up, f"ff_sig{j}", [P, T * P], F32) for j in range(2)]
            hid = [chip.sb(up, f"ff_hid{j}", [P, T * P], F32) for j in range(2)]
            unpack = Unpacker(chip, up, "fu", COLS)
            turn = [chip.ps(up, f"ff_turn{g}", [P, HALF], F32) for g in range(2)]
            acc = [[chip.ps(up, f"ff_acc{j}{g}", [P, T * P], F32) for g in range(2)] for j in range(2)]
            raw_loaded, cleared, scaled = chip.sem("ff_raw_loaded"), chip.sem("ff_cleared"), chip.sem("ff_scaled")
            rows_loaded, tail_cleared, turned = chip.sem("ff_rows_loaded"), chip.sem("ff_tail"), chip.sem("ff_turned")
            summed, sig_ready, hid_step = chip.sem("ff_summed"), chip.sem("ff_sig"), chip.sem("ff_hid_steps")
            hid_ready, h_hi_ready, h_lo_ready = chip.sem("ff_hid"), chip.sem("ff_h_hi"), chip.sem("ff_h_lo")
            SUMMED0, HID0, HLO0 = 2 * QC, QC, QC
            block = up.enter_context(nc.Block())

            def each_block(eng, body):
                with eng.Fori(0, NB - 1) as b:
                    body(b, False)
                body(NB - 1, True)

            @block.sync
            def _(sp):
                for k in range(8):
                    sp.dma_start(raw[k * GROUP_ROWS:(k + 1) * GROUP_ROWS, :],
                                 gu_scale_d[k].rearrange("(a n) -> a n", a=1).to_broadcast((GROUP_ROWS, 2 * INNER)))\
                        .then_inc(raw_loaded, 16)

                def load(b, parts):
                    for g in range(2):
                        src = gu_d[bass.ds(b * D + g * INNER, WORD * parts), :].rearrange("(w j) c -> w j c", j=WORD)
                        sp.dma_start(rows[g][0:parts], src).then_inc(rows_loaded, 16)

                load(0, P)
                sp.wait_ge(turned, 2 * NQ)
                load(1, P)
                sp.wait_ge(tail_cleared, 2)
                load(NB - 1, LAST)
                sp.wait_ge(dn_cleared, 2)
                sp.dma_start(dn_rows[:, :, 0:INNER // WORD], dn_d.rearrange("(a p) c -> p a c", p=P)).then_inc(dn_loaded, 16)
                for k in range(INNER // P):
                    b, at = k // 8, (k % 8) * GROUP_ROWS
                    sp.dma_start(dn_scale[at:at + GROUP_ROWS, b, :],
                                 dn_scale_d[k].rearrange("(a n) -> a n", a=1).to_broadcast((GROUP_ROWS, D)))\
                        .then_inc(dn_loaded, 16)
                sp.wait_ge(dn_loaded, 16 * (1 + INNER // P))

            @block.tensor
            def _(pe):
                pe.sem_inc(summed, SUMMED0)

                def turn_words(K, b, q, first):
                    if q == 0:
                        pe.wait_ge(rows_loaded, 32 * b + 32)
                    for g in range(2):
                        if not first:
                            pe.wait_ge(unpack.taken, 2 * K + g - 1)
                        for j in range(QC):
                            last = nc.tensor.transpose(turn[g][:, j * P:(j + 1) * P],
                                                       rows[g][:, QC * q + j, :].bitcast(F32), ident32[:])
                        last.then_inc(turned, 1)

                def body(b, last_block):
                    for q in range(NQ):
                        K = NQ * b + q
                        if q + 1 < NQ:
                            turn_words(K + 1, b, q + 1, False)
                        elif not last_block:
                            turn_words(K + 1, b + 1, 0, False)
                        pe.wait_ge(unpack.lo_ready, unpack.LO0 + 2 * K + 2)
                        for j in range(QC):
                            pe.wait_ge(hid_ready, HID0 + QC * (K - 1) + j + 1)
                            for g in range(2):
                                cols = slice(g * COLS + j * P, g * COLS + (j + 1) * P)
                                for k in range(WORD):
                                    for n, (w, v) in enumerate(((w_hi, xt_hi), (w_hi, xt_lo), (w_lo, xt_hi))):
                                        last = nc.tensor.matmul(acc[j][g][:], w[q % 2][:, k, cols], v[:, k, :],
                                                                start=(k == 0 and n == 0),
                                                                stop=(k == WORD - 1 and n == 2))
                            last.then_inc(summed, 1)

                turn_words(0, 0, 0, True)
                each_block(pe, body)

            @block.vector
            def _(dve):
                dve.sem_inc(hid_ready, HID0)
                nc.vector.memset(scale[:], 0.0).then_inc(cleared, 1)
                nc.vector.memset(dn_rows[:], 0).then_inc(dn_cleared, 1)
                nc.vector.memset(dn_scale[:], 0.0).then_inc(dn_cleared, 1)
                dve.wait_ge(cleared, 1)
                dve.wait_ge(raw_loaded, 16 * 8)
                for g in range(2):
                    for b in range(NB):
                        n = P if b < NB - 1 else LAST
                        at = g * INNER + b * D
                        nc.vector.tensor_scalar(scale[:, g * NB + b, :, 0:n],
                                                raw[:, at:at + WORD * n].rearrange("p (w j) -> p j w", j=WORD),
                                                SC_SCALE, None, ALU.mult).then_inc(scaled, 1)
                dve.wait_ge(scaled, 2 * NB)

                def unit(K, b, q, g):
                    dve.wait_ge(turned, 2 * K + g + 1)
                    at = scale[:, bass.ds(g * NB + b, 1), QC * q:QC * q + QC, :].rearrange("p a j w -> p (a j w)")
                    unpack.product(dve, 2 * K + g, g, turn[g][:, 0:COLS].bitcast(I32), at)

                def hidden(K, j):
                    dve.wait_ge(sig_ready, QC * K + j + 1)
                    nc.vector.scalar_tensor_tensor(out=sig[j][:], in0=acc[j][0][:], scalar=UP_OUT, in1=sig[j][:],
                                                   op0=ALU.mult, op1=ALU.mult).then_inc(hid_step, 1)
                    dve.wait_ge(hid_step, QC * K + j + 1)
                    dve.wait_ge(h_lo_ready, HLO0 + QC * (K - 1) + j + 1)
                    nc.vector.scalar_tensor_tensor(out=hid[j][:], in0=acc[j][1][:], scalar=UP_OUT * H_SCALE,
                                                   in1=sig[j][:], op0=ALU.mult, op1=ALU.mult).then_inc(hid_ready, 1)

                def clear_tail():
                    dve.wait_ge(turned, 2 * NQ * (NB - 1))
                    for g in range(2):
                        nc.vector.memset(rows[g][LAST:P], 0).then_inc(tail_cleared, 1)

                def body(b, last_block):
                    for q in range(NQ):
                        K = NQ * b + q
                        for g in range(2):
                            if q + 1 < NQ:
                                unit(K + 1, b, q + 1, g)
                            elif not last_block:
                                unit(K + 1, b + 1, 0, g)
                            hidden(K, g)

                unit(0, 0, 0, 0)
                unit(0, 0, 0, 1)
                body(0, False)
                for q in range(NQ):
                    K = NQ + q
                    for g in range(2):
                        if q + 1 < NQ:
                            unit(K + 1, 1, q + 1, g)
                        else:
                            if g == 0:
                                clear_tail()
                            unit(K + 1, 2, 0, g)
                        hidden(K, g)
                body(NB - 1, True)
                dve.wait_ge(hid_ready, HID0 + NB * WORD)

            @block.scalar
            def _(act):
                def unit(K, q, g):
                    act.wait_ge(summed, SUMMED0 + QC * (K - 1))
                    unpack.high(act, 2 * K + g, g, w_hi[q % 2][:, :, g * COLS:(g + 1) * COLS])

                def hidden(b, q, j):
                    K = NQ * b + q
                    act.wait_ge(summed, SUMMED0 + QC * K + j + 1)
                    act.wait_ge(hid_ready, HID0 + QC * (K - 1) + j + 1)
                    nc.scalar.activation(sig[j][:], acc[j][0][:], ACT.Sigmoid, scale=UP_OUT).then_inc(sig_ready, 1)
                    act.wait_ge(hid_ready, HID0 + QC * K + j + 1)
                    nc.scalar.activation(h_hi[:, bass.ds(b * WORD + QC * q + j, 1), :].rearrange("p a n -> p (a n)"),
                                         hid[j][:], ACT.Copy).then_inc(h_hi_ready, 1)

                def body(b, last_block):
                    for q in range(NQ):
                        for g in range(2):
                            if not (last_block and q + 1 == NQ):
                                unit(NQ * b + q + 1, (q + 1) % NQ, g)
                            hidden(b, q, g)

                unit(0, 0, 0)
                unit(0, 0, 1)
                each_block(act, body)

            @block.gpsimd
            def _(pool):
                pool.sem_inc(unpack.lo_ready, unpack.LO0)
                pool.sem_inc(h_lo_ready, HLO0)

                def unit(K, q, g):
                    cols = slice(g * COLS, (g + 1) * COLS)
                    unpack.low(pool, 2 * K + g, g, w_hi[q % 2][:, :, cols], w_lo[q % 2][:, :, cols])

                def hidden(b, q, j):
                    pool.wait_ge(h_hi_ready, QC * (NQ * b + q) + j + 1)
                    at = bass.ds(b * WORD + QC * q + j, 1)
                    nc.gpsimd.tensor_tensor(h_lo[:, at, :].rearrange("p a n -> p (a n)"), hid[j][:],
                                            h_hi[:, at, :].rearrange("p a n -> p (a n)"),
                                            ALU.subtract).then_inc(h_lo_ready, 1)

                def body(b, last_block):
                    for q in range(NQ):
                        for g in range(2):
                            if not (last_block and q + 1 == NQ):
                                unit(NQ * b + q + 1, (q + 1) % NQ, g)
                            hidden(b, q, g)

                unit(0, 0, 0)
                unit(0, 0, 1)
                each_block(pool, body)
                pool.wait_ge(h_lo_ready, HLO0 + NB * WORD)

        y = chip.sb(ctx, "ff_y", [P, T, D], F32)
        sq = chip.sb(ctx, "ff_sq", [P, D], F32)
        small = chip.sb(ctx, "ff_small", [P, 5, T], F32)
        unpack = Unpacker(chip, ctx, "fd", COLS)
        turn = [chip.ps(ctx, f"fd_turn{g}", [P, HALF], F32) for g in range(2)]
        acc = [chip.ps(ctx, f"fd_acc{t}", [P, HALF], F32) for t in range(T)]
        turned, summed, taken = chip.sem("fd_turned"), chip.sem("fd_summed"), chip.sem("fd_y")
        squared, mean_ready, root_ready = chip.sem("fd_squared"), chip.sem("fd_mean"), chip.sem("fd_root")
        norm_step, out_ready, stored = chip.sem("fd_norm_steps"), chip.sem("fd_out"), chip.sem("fd_stored")
        chunks = [(half, b) for half in range(2) for b in range(NB)]
        block = ctx.enter_context(nc.Block())

        @block.tensor
        def _(pe):
            def turn_words(L):
                half, b = chunks[L]
                for g in range(2):
                    if L >= 1:
                        pe.wait_ge(unpack.taken, 2 * L + g - 1)
                    for j in range(QC):
                        words = dn_rows[:, 4 * half + QC * g + j, b * P:(b + 1) * P]
                        last = nc.tensor.transpose(turn[g][:, j * P:(j + 1) * P], words.bitcast(F32), ident32[:])
                    last.then_inc(turned, 1)

            turn_words(0)
            for L, (half, b) in enumerate(chunks):
                if L + 1 < len(chunks):
                    turn_words(L + 1)
                pe.wait_ge(unpack.lo_ready, unpack.LO0 + 2 * L + 2)
                for t in range(T):
                    if half == 1 and b == 0:
                        pe.wait_ge(taken, t + 1)
                    for k in range(WORD):
                        for n, (v, w) in enumerate(((h_hi, w_hi), (h_hi, w_lo), (h_lo, w_hi))):
                            last = nc.tensor.matmul(acc[t][:], v[:, b * WORD + k, t * P:(t + 1) * P], w[L % 2][:, k, :],
                                                    start=(b == 0 and k == 0 and n == 0),
                                                    stop=(b == NB - 1 and k == WORD - 1 and n == 2))
                    last.then_inc(summed, 1)

        @block.vector
        def _(dve):
            def units(L):
                half, b = chunks[L]
                for g in range(2):
                    dve.wait_ge(turned, 2 * L + g + 1)
                    at = half * HALF + g * COLS
                    unpack.product(dve, 2 * L + g, g, turn[g][:, 0:COLS].bitcast(I32), sc_down[:, b, at:at + COLS])

            sc_down = dn_scale
            nc.vector.tensor_scalar(dn_scale[:], dn_scale[:], SC_SCALE, None, ALU.mult).then_inc(dn_scaled, 1)
            dve.wait_ge(dn_scaled, 1)
            units(0)
            for L, (half, b) in enumerate(chunks):
                if L + 1 < len(chunks):
                    units(L + 1)
                if b == NB - 1:
                    for t in range(T):
                        dve.wait_ge(summed, T * L + t + 1)
                        nc.vector.tensor_scalar(y[:, t, half * HALF:(half + 1) * HALF], acc[t][:], DOWN_OUT, None,
                                                ALU.mult).then_inc(taken, 1)
            dve.wait_ge(squared, T)
            var, root, tmp, rstd = (small[:, k, :] for k in range(1, 5))
            nc.vector.tensor_scalar(var, small[:, 0, :], 1.0 / D, RMS_EPS, ALU.mult, ALU.add).then_inc(mean_ready, 1)
            dve.wait_ge(mean_ready, 1)
            rsqrt_steps(nc, dve, norm_step, root_ready, 0, var, root, tmp, rstd)
            for t in range(T):
                nc.vector.scalar_tensor_tensor(out=y[:, t, :], in0=y[:, t, :], scalar=rstd[:, t:t + 1],
                                               in1=x[:, t, :], op0=ALU.mult, op1=ALU.add).then_inc(out_ready, 1)

        @block.scalar
        def _(act):
            for L in range(len(chunks)):
                for g in range(2):
                    if L >= 2:
                        act.wait_ge(summed, T * (L - 1))
                    unpack.high(act, 2 * L + g, g, w_hi[L % 2][:, :, g * COLS:(g + 1) * COLS])
            for t in range(T):
                act.wait_ge(taken, T + t + 1)
                if t:
                    act.wait_ge(squared, t)
                nc.scalar.activation(sq[:], y[:, t, :], ACT.Square, accum_out=small[:, 0, t:t + 1]).then_inc(squared, 1)
            act.wait_ge(mean_ready, 1)
            nc.scalar.activation(small[:, 2, :], small[:, 1, :], ACT.Sqrt).then_inc(root_ready, 1)

        @block.gpsimd
        def _(pool):
            pool.sem_inc(unpack.lo_ready, unpack.LO0)
            for L in range(len(chunks)):
                for g in range(2):
                    cols = slice(g * COLS, (g + 1) * COLS)
                    unpack.low(pool, 2 * L + g, g, w_hi[L % 2][:, :, cols], w_lo[L % 2][:, :, cols])

        @block.sync
        def _(sp):
            for t in range(T):
                sp.wait_ge(out_ready, t + 1)
                sp.dma_start(out_d[t], y[:, t, :]).then_inc(stored, 16)
            sp.wait_ge(stored, 16 * T)


def build(nc, a, out_d):
    chip = Chip(nc)
    kt_d = nc.dram_tensor("keys_turned", (HEADS, P, NKV), F16, kind="Internal").ap()
    v_d = nc.dram_tensor("values", (HEADS, P, KVT, HD), F32, kind="Internal").ap()
    scale_d = nc.dram_tensor("value_steps", (D,), F32, kind="Internal").ap()
    x_d = a["x"].rearrange("b p n -> p b n")
    with chip.all, ExitStack() as whole:
        ident32 = chip.sb(whole, "ident32", [P, P], F32)
        ident16 = chip.sb(whole, "ident16", [P, P], F16)
        make_constants(chip, a["ident"], ident32, ident16)
        o = chip.sb(whole, "o", [P, T, D], F32)
        with ExitStack() as cross:
            q_t = chip.sb(cross, "q_t", [P, HEADS, T * P], F16)
            exp_scale = chip.sb(cross, "exp_scale", [P, HEADS, T], F32)
            v_scale = chip.sb(cross, "v_scale", [P, D], F32)
            v_inv = chip.sb(cross, "v_inv", [P, D], F32)
            vmax = v_inv
            with ExitStack() as c:
                x = chip.sb(c, "x_in", [P, T, D], F32)
                bias = chip.sb(c, "q_bias", [P, D], F32)
                xt_hi = chip.sb(c, "q_xthi", [P, KD, T * P], F16)
                xt_lo = chip.sb(c, "q_xtlo", [P, KD, T * P], F16)
                q = chip.sb(c, "q", [P, T, D], F32)
                load_rows(chip, (x[:], x_d), (bias[:], flat_bcast(a["bq"], D)))
                normalise(chip, "n1", x, q)
                transpose_split(chip, "t1", lambda t, k: q[:, t, k * P:(k + 1) * P], xt_hi, xt_lo, ident32)
                project(chip, "pq", xt_hi, xt_lo, a["wq"], 1, lambda w, t, h: bias[:, h * HALF:(h + 1) * HALF],
                        lambda w, t, h: q[:, t, h * HALF:(h + 1) * HALF])
                quantise_queries(chip, q, q_t, exp_scale, ident16)
            keys_and_values(chip, a["ctx"], a["wkv"], a["bkv"], kt_d, v_d, vmax, ident32, ident16)
            value_scales(chip, vmax, scale_d, v_scale, v_inv, ident32)
            attend_quantised(chip, q_t, exp_scale, kt_d, v_d, v_scale, v_inv, o, ident16)
        x = chip.sb(whole, "x", [P, T, D], F32)
        load_rows(chip, (x[:], x_d))

        def add_projection(tag, w_d, b_d):
            with ExitStack() as c:
                bias = chip.sb(c, f"{tag}_bias", [P, D], F32)
                xt_hi = chip.sb(c, f"{tag}_xthi", [P, KD, T * P], F16)
                xt_lo = chip.sb(c, f"{tag}_xtlo", [P, KD, T * P], F16)
                load_rows(chip, (bias[:], flat_bcast(b_d, D)))
                add_rows(chip, f"{tag}_xb", x, x, bias)
                transpose_split(chip, f"{tag}_t", lambda t, k: o[:, t, k * P:(k + 1) * P], xt_hi, xt_lo, ident32)
                project(chip, tag, xt_hi, xt_lo, w_d, 1, lambda w, t, h: x[:, t, h * HALF:(h + 1) * HALF],
                        lambda w, t, h: x[:, t, h * HALF:(h + 1) * HALF])

        add_projection("pp", a["wp"], a["bp"])
        with ExitStack() as c:
            y = [chip.sb(c, f"y{w}", [P, T, D], F32) for w in range(3)]
            with ExitStack() as cc:
                bias = chip.sb(cc, "qkv_bias", [P, 3 * D], F32)
                xt_hi = chip.sb(cc, "s_xthi", [P, KD, T * P], F16)
                xt_lo = chip.sb(cc, "s_xtlo", [P, KD, T * P], F16)
                load_rows(chip, (bias[:], flat_bcast(a["bqkv"], 3 * D)))
                normalise(chip, "n2", x, o)
                transpose_split(chip, "t2", lambda t, k: o[:, t, k * P:(k + 1) * P], xt_hi, xt_lo, ident32)
                project(chip, "ps", xt_hi, xt_lo, a["wqkv"], 3,
                        lambda w, t, h: bias[:, w * D + h * HALF:w * D + (h + 1) * HALF],
                        lambda w, t, h: y[w][:, t, h * HALF:(h + 1) * HALF])
            with ExitStack() as cc:
                tables = chip.sb(cc, "rope_tables", [P, 2, HD], F32)
                mask = chip.sb(cc, "mask", [P, P], F32)
                load_rows(chip, (tables[:], a["rope"].rearrange("c p d -> p c d")), (mask[:], a["mask"]))
                rotate(chip, y[0], y[1], tables[:, 0, :], tables[:, 1, :])
                attend_causal(chip, y[0], y[1], y[2], mask, o, ident32)
        add_projection("po", a["wo"], a["bo"])
        with ExitStack() as c:
            xt_hi = chip.sb(c, "f_xthi", [P, KD, T * P], F16)
            xt_lo = chip.sb(c, "f_xtlo", [P, KD, T * P], F16)
            normalise(chip, "n3", x, o)
            transpose_split(chip, "t3", lambda t, k: o[:, t, :].rearrange("p (w j) -> p j w", j=WORD)[:, k, :],
                            xt_hi, xt_lo, ident32)
            feed_forward(chip, xt_hi, xt_lo, a["gu"], a["gu_scale"], a["dn"], a["dn_scale"], x, o, out_d, ident32)


def kernel(x, ctx_2048, L0_xattn_Wq, L0_xattn_bq, L0_xattn_Wkv, L0_xattn_bkv, L0_xattn_Wp, L0_xattn_bp,
           L0_attn_Wq, L0_attn_bq, L0_attn_Wk, L0_attn_bk, L0_attn_Wv, L0_attn_bv, L0_attn_Wo, L0_attn_bo,
           L0_ffn_gate_up_packed, L0_ffn_gate_up_scales, L0_ffn_down_packed, L0_ffn_down_scales):
    import concourse.bacc as bacc
    from concourse.bass_utils import run_bass_kernel_spmd

    pos = np.arange(S, dtype=np.float32)[:, None]
    exps = -np.arange(0, HD, 2, dtype=np.float32) / np.float32(HD)
    angles = pos * np.repeat(np.power(np.float32(10000.0), exps), 2)[None, :]
    cos, sin = np.cos(angles), np.sin(angles)
    sin[:, 0::2] *= -1.0
    mask = np.where(np.triu(np.ones((S, S), bool), k=1), np.float32(-1e30), np.float32(0.0)).astype(np.float32)
    arrays = {
        "x": np.asarray(x), "ctx": np.asarray(ctx_2048).reshape(KVT, P, D),
        "wq": np.asarray(L0_xattn_Wq)[None], "bq": np.asarray(L0_xattn_bq),
        "wkv": np.asarray(L0_xattn_Wkv), "bkv": np.asarray(L0_xattn_bkv),
        "wp": np.asarray(L0_xattn_Wp)[None], "bp": np.asarray(L0_xattn_bp),
        "wqkv": np.stack([np.asarray(L0_attn_Wq), np.asarray(L0_attn_Wk), np.asarray(L0_attn_Wv)]),
        "bqkv": np.concatenate([np.asarray(L0_attn_bq), np.asarray(L0_attn_bk), np.asarray(L0_attn_bv)]),
        "wo": np.asarray(L0_attn_Wo)[None], "bo": np.asarray(L0_attn_bo),
        "gu": np.asarray(L0_ffn_gate_up_packed), "gu_scale": np.asarray(L0_ffn_gate_up_scales),
        "dn": np.asarray(L0_ffn_down_packed), "dn_scale": np.asarray(L0_ffn_down_scales),
        "rope": np.stack([cos, sin]).astype(np.float32), "mask": mask, "ident": np.eye(P, dtype=np.float32),
    }
    nc = bacc.Bacc("TRN2", target_bir_lowering=False, num_devices=1)
    feeds, aps = {}, {}
    for name, v in arrays.items():
        feeds[f"in_{name}"] = v = np.ascontiguousarray(v)
        aps[name] = nc.dram_tensor(f"in_{name}", v.shape, mybir.dt.from_np(v.dtype), kind="ExternalInput").ap()
    out_d = nc.dram_tensor("out", (B, S, D), F32, kind="ExternalOutput").ap()
    build(nc, aps, out_d)
    r = run_bass_kernel_spmd(nc, [feeds], core_ids=[0])
    return r.results[0]["out"]
```

```python
from contextlib import ExitStack

import numpy as np

import concourse.bass as bass
from concourse import mybir

ALU = mybir.AluOpType
ACT = mybir.ActivationFunctionType
AX = mybir.AxisListType
F32 = mybir.dt.float32
F16 = mybir.dt.float16
U16 = mybir.dt.uint16
I32 = mybir.dt.int32

P = 128
B, S, D = 4, 128, 1024
T = B * S // P
HEADS, HD = 16, 64
KD = D // P
HALF = 512
NKV = 4 * 2048
KVT = NKV // P
X_SCALE, W_SCALE, K_SCALE = 16.0, 256.0, 64.0
UNSCALE = 1.0 / (X_SCALE * W_SCALE)
MAGIC = 1.5 * 2.0 ** 23
LEVELS = 127.0
LN_EPS, RMS_EPS = 1e-5, 1e-6
INNER = 2816
WORD = 8
NB = 3
LAST = (INNER - 2 * D) // WORD
GROUP_ROWS = 16
SC_SCALE = 4096.0
NIB_SCALE = 2.0 ** -14
H_SCALE = 2.0 ** -10


def flat_bcast(row, n):
    return row.rearrange("(a n) -> a n", a=1).to_broadcast((P, n))


class Chip:

    def __init__(self, nc):
        self.nc = nc
        self.all = ExitStack()
        self.rows_loaded, self.loads = self.sem("rows_loaded"), 0
        self.turn_sems, self.turns = [self.sem(f"turn_{n}") for n in ("turned", "hi", "lo")], 0
        self.row_added, self.rows_added = self.sem("row_added"), 0
        self.norm_sems, self.norms = [self.sem(f"norm_{n}") for n in ("steps", "var", "root", "rows")], 0

    def sem(self, name):
        return self.all.enter_context(self.nc.semaphore(name))

    def sb(self, ctx, name, shape, dt):
        return ctx.enter_context(self.nc.sbuf_tensor(name, shape, dt))

    def ps(self, ctx, name, shape, dt):
        return ctx.enter_context(self.nc.psum_tensor(name, shape, dt))


def start(chip, ident_d, ident32, ident16, x_d, x, x_loaded):
    nc = chip.nc
    loaded, made = chip.sem("ident_loaded"), chip.sem("ident_made")
    with nc.Block() as block:
        @block.sync
        def _(sp):
            sp.dma_start(ident32[:], ident_d).then_inc(loaded, 16)
            sp.dma_start(x[:], x_d).then_inc(x_loaded, 16)

        @block.vector
        def _(dve):
            dve.wait_ge(loaded, 16)
            nc.vector.tensor_copy(ident16[:], ident32[:]).then_inc(made, 1)
            dve.wait_ge(made, 1)


def start_loads(chip, panels, *pairs, apart=()):
    with chip.nc.Block() as block:
        @block.sync
        def _(sp):
            for n in range(2):
                panels.load(sp, n)
            for dst, src in pairs:
                sp.dma_start(dst, src).then_inc(chip.rows_loaded, 16)
            for dst, src, loaded in apart:
                sp.dma_start(dst, src).then_inc(loaded, 16)
    chip.loads += len(pairs)


def rsqrt_steps(nc, dve, done, n, root_ready, roots, var, root, tmp, rstd):
    dve.wait_ge(root_ready, roots)
    nc.vector.reciprocal(tmp, root).then_inc(done, 1)
    dve.wait_ge(done, n + 1)
    nc.vector.tensor_tensor(tmp, tmp, var, ALU.mult).then_inc(done, 1)
    dve.wait_ge(done, n + 2)
    nc.vector.tensor_tensor(tmp, tmp, root, ALU.add).then_inc(done, 1)
    dve.wait_ge(done, n + 3)
    nc.vector.tensor_scalar(tmp, tmp, 0.5, None, ALU.mult).then_inc(done, 1)
    dve.wait_ge(done, n + 4)
    nc.vector.reciprocal(rstd, tmp).then_inc(done, 1)
    dve.wait_ge(done, n + 5)


def row_stats_of(chip, ctx):
    return chip.sb(ctx, f"stats{chip.norms}_{chip.turns}", [P, T, 2, chip.nc.vector.BN_STATS_DIM], F32)


def row_stats(nc, step, stats, rows, t):
    for h in range(2):
        nc.vector.bn_stats(stats[:, t, h, :], rows[:, t, h * HALF:(h + 1) * HALF]).then_inc(step, 1)


class Turner:

    STEPS = 3 * T + 5

    def __init__(self, chip, ctx, banks, src, block_of, xt_hi, xt_lo, ident32, normed=None, stats=None,
                 loaded=None):
        self.nc, self.banks, self.src, self.block_of = chip.nc, banks, src, block_of
        self.xt_hi, self.xt_lo, self.ident32, self.normed, self.loaded = xt_hi, xt_lo, ident32, normed, loaded
        self.turned, self.hi_ready, self.lo_ready = chip.turn_sems
        self.step, self.var_ready, self.root_ready, self.rows_ready = chip.norm_sems
        self.units = [(t, h) for t in range(T) for h in range(2)]
        self.first, self.norms = chip.turns * len(self.units), chip.norms
        if normed is not None:
            self.stats, self.have_stats = stats or row_stats_of(chip, ctx), stats is not None
            self.aggr = chip.sb(ctx, f"aggr{chip.norms}", [P, T, chip.nc.vector.BN_AGGR_DIM], F32)
            self.small = chip.sb(ctx, f"norm_small{chip.norms}", [P, 4, T], F32)
        chip.turns += 1
        chip.norms += normed is not None

    def bank(self, n):
        return self.banks[n % len(self.banks)]

    def tensor(self, pe):
        for n, (t, h) in enumerate(self.units):
            if self.normed is not None and h == 0:
                pe.wait_ge(self.rows_ready, self.norms * T + t + 1)
            if n >= len(self.banks):
                pe.wait_ge(self.lo_ready, self.first + n - len(self.banks) + 1)
            for k in range(4):
                last = self.nc.tensor.transpose(self.bank(n)[:, k * P:(k + 1) * P],
                                                self.block_of(self.src, t, 4 * h + k), self.ident32[:])
            last.then_inc(self.turned, 1)

    def wait_tile(self, pe, t):
        pe.wait_ge(self.lo_ready, self.first + 2 * t + 2)

    def part(self, t, h):
        return slice(None), slice(4 * h, 4 * h + 4), slice(t * P, (t + 1) * P)

    def blocks(self, n):
        return self.bank(n)[:].rearrange("p (k n) -> p k n", n=P)

    def scalar(self, act):
        if self.normed is not None:
            act.wait_ge(self.var_ready, self.norms + 1)
            self.nc.scalar.activation(self.small[:, 1, :], self.small[:, 0, :], ACT.Sqrt).then_inc(self.root_ready, 1)
        for n, (t, h) in enumerate(self.units):
            act.wait_ge(self.turned, self.first + n + 1)
            self.nc.scalar.activation(self.xt_hi[self.part(t, h)], self.blocks(n), ACT.Copy,
                                      scale=X_SCALE).then_inc(self.hi_ready, 1)

    def vector(self, dve):
        nc = self.nc
        if self.normed is not None:
            at = self.norms * self.STEPS
            var, root, tmp, rstd = (self.small[:, k, :] for k in range(4))
            if self.loaded is not None:
                dve.wait_ge(self.loaded, 16)
            if not self.have_stats:
                for t in range(T):
                    row_stats(nc, self.step, self.stats, self.normed, t)
            dve.wait_ge(self.step, at + 2 * T)
            for t in range(T):
                nc.vector.bn_aggr(self.aggr[:, t, :], self.stats[:, t, :, :]).then_inc(self.step, 1)
            dve.wait_ge(self.step, at + 3 * T)
            nc.vector.tensor_scalar(var, self.aggr[:, :, 1], LN_EPS, None, ALU.add).then_inc(self.var_ready, 1)
            dve.wait_ge(self.var_ready, self.norms + 1)
            rsqrt_steps(nc, dve, self.step, at + 3 * T, self.root_ready, self.norms + 1, var, root, tmp, rstd)
            for t in range(T):
                nc.vector.tensor_scalar(self.src[:, t, :], self.normed[:, t, :], self.aggr[:, t, 0:1],
                                        rstd[:, t:t + 1], ALU.subtract, ALU.mult).then_inc(self.rows_ready, 1)
        for n, (t, h) in enumerate(self.units):
            dve.wait_ge(self.hi_ready, self.first + n + 1)
            part = self.part(t, h)
            nc.vector.scalar_tensor_tensor(out=self.xt_lo[part], in0=self.blocks(n), scalar=X_SCALE,
                                           in1=self.xt_hi[part], op0=ALU.mult,
                                           op1=ALU.subtract).then_inc(self.lo_ready, 1)


class WeightPanels:

    def __init__(self, chip, ctx, tag, sources, to=None):
        self.nc, self.sources = chip.nc, sources
        self.loaded = [chip.sem(f"{tag}_loaded{j}") for j in range(2)]
        self.hi_ready, self.lo_ready = chip.sem(f"{tag}_hi"), chip.sem(f"{tag}_lo")
        self.summed, self.taken = chip.sem(f"{tag}_summed"), chip.sem(f"{tag}_taken")
        self.stage = [chip.sb(ctx, f"{tag}_stage{j}", [P, KD, HALF], F32) for j in range(2)]
        to = to or {}
        self.in_ring = [n not in to for n in range(len(sources))]
        ring = {j: [chip.sb(ctx, f"{tag}_ring{q}{j}", [P, KD, HALF], F16) for q in range(2)]
                for j in sorted({n % 2 for n in range(len(sources)) if self.in_ring[n]})}
        self.parts = [to[n] if n in to else [r[:] for r in ring[n % 2]] for n in range(len(sources))]
        self.next_load = 0

    def load(self, sp, n):
        assert n == self.next_load
        self.next_load += 1
        if n >= 2:
            sp.wait_ge(self.lo_ready, n - 1)
        sp.dma_start(self.stage[n % 2][:], self.sources[n].rearrange("(k p) n -> p k n", p=P))\
            .then_inc(self.loaded[n % 2], 16)

    def high(self, act, n):
        act.wait_ge(self.loaded[n % 2], 16 * (n // 2 + 1))
        if n >= 2 and self.in_ring[n]:
            act.wait_ge(self.summed, T * (n - 1))
        self.nc.scalar.activation(self.parts[n][0], self.stage[n % 2][:], ACT.Copy, scale=W_SCALE)\
            .then_inc(self.hi_ready, 1)

    def low(self, dve, n):
        dve.wait_ge(self.hi_ready, n + 1)
        self.nc.vector.scalar_tensor_tensor(out=self.parts[n][1], in0=self.stage[n % 2][:], scalar=W_SCALE,
                                            in1=self.parts[n][0], op0=ALU.mult,
                                            op1=ALU.subtract).then_inc(self.lo_ready, 1)


def project(chip, tag, panels, first, count, split_first, split_after, rows, addend, out, added=None, beside=None,
            stats=None):
    nc = chip.nc
    splits = list(split_first) + [m for n in range(count) for m in split_after[n]]
    with ExitStack() as ctx:
        acc = [chip.ps(ctx, f"{tag}_acc{n}", [P, HALF], F32) for n in range(2 * T)]
        turner = Turner(chip, ctx, acc[T:], *rows)
        block = ctx.enter_context(nc.Block())

        @block.sync
        def _(sp):
            last = splits[-1] if splits else panels.next_load - 3
            while panels.next_load < min(len(panels.sources), last + 3):
                panels.load(sp, panels.next_load)

        @block.scalar
        def _(act):
            turner.scalar(act)
            for m in splits:
                panels.high(act, m)

        @block.vector
        def _(dve):
            turner.vector(dve)
            for m in split_first:
                panels.low(dve, m)
            dve.wait_ge(chip.rows_loaded, 16 * chip.loads)
            if added is not None:
                dve.wait_ge(chip.row_added, chip.rows_added + 1)
            for n in range(count):
                for t in range(T):
                    dve.wait_ge(panels.summed, T * (first + n) + t + 1)
                    nc.vector.scalar_tensor_tensor(out=out(n, t), in0=acc[T * (n % 2) + t][:], scalar=UNSCALE,
                                                   in1=addend(n, t), op0=ALU.mult,
                                                   op1=ALU.add).then_inc(panels.taken, 1)
                    if stats is not None and n == count - 1 and t > 0:
                        dve.wait_ge(panels.taken, T * (first + n) + t)
                        row_stats(nc, chip.norm_sems[0], *stats, t - 1)
                for m in split_after[n]:
                    panels.low(dve, m)
            dve.wait_ge(panels.taken, T * (first + count))
            if stats is not None:
                row_stats(nc, chip.norm_sems[0], *stats, T - 1)

        @block.tensor
        def _(pe):
            turner.tensor(pe)
            for n in range(count):
                w_hi, w_lo = panels.parts[first + n]
                pe.wait_ge(panels.lo_ready, first + n + 1)
                for t in range(T):
                    if n == 0:
                        turner.wait_tile(pe, t)
                    if n >= 2:
                        pe.wait_ge(panels.taken, T * (first + n - 2) + t + 1)
                    for k in range(KD):
                        tok = slice(t * P, (t + 1) * P)
                        for q, (a, b) in enumerate(((turner.xt_hi, w_hi), (turner.xt_hi, w_lo), (turner.xt_lo, w_hi))):
                            last = nc.tensor.matmul(acc[T * (n % 2) + t][:], a[:, k, tok], b[:, k, :],
                                                    start=(k == 0 and q == 0), stop=(k == KD - 1 and q == 2))
                    last.then_inc(panels.summed, 1)

        @block.gpsimd
        def _(pool):
            if added is not None:
                rows_, row = added
                pool.wait_ge(chip.rows_loaded, 16 * chip.loads)
                nc.gpsimd.tensor_tensor(rows_[:], rows_[:], row.unsqueeze(1).to_broadcast((P, T, D)),
                                        ALU.add).then_inc(chip.row_added, 1)
            if beside is not None:
                beside(pool)
    chip.rows_added += added is not None


def heads_of(ap):
    return ap.rearrange("p (h d) -> p h d", d=HD)


def per_head(ap):
    return ap.unsqueeze(2).to_broadcast((P, HEADS, HD))


class Queries:

    def __init__(self, chip, ctx, q, exp_scale, twice):
        self.nc, self.q, self.exp_scale, self.twice = chip.nc, q, exp_scale, twice
        self.amax, self.scale, self.inv = (chip.sb(ctx, f"qq_{n}", [P, T, HEADS], F32) for n in ("amax", "scale", "inv"))
        self.magic = chip.sb(ctx, "qq_magic", [P, 1], F32)
        self.scaled, self.step = chip.sem("qq_scaled"), chip.sem("qq_steps")

    def vector(self, dve):
        nc = self.nc
        nc.vector.tensor_scalar(self.q[:], self.q[:], HD ** -0.5, None, ALU.mult).then_inc(self.scaled, 1)
        dve.wait_ge(self.scaled, 1)
        nc.vector.tensor_reduce(self.amax[:], self.q[:].rearrange("p t (h d) -> p t h d", d=HD), AX.X, ALU.max,
                                apply_absolute_value=True).then_inc(self.scaled, 1)
        dve.wait_ge(self.scaled, 2)
        nc.vector.tensor_scalar(self.scale[:], self.amax[:], 1.0 / LEVELS, 1e-8, ALU.mult, ALU.max)\
            .then_inc(self.scaled, 1)
        dve.wait_ge(self.scaled, 3)
        nc.vector.reciprocal(self.inv[:], self.scale[:]).then_inc(self.scaled, 1)
        nc.vector.tensor_scalar(self.exp_scale[:].rearrange("p h t -> p t h"), self.scale[:], 1.0 / K_SCALE, None,
                                ALU.mult).then_inc(self.scaled, 1)

    def gpsimd(self, pool):
        nc, q, step = self.nc, self.q, self.step
        nc.gpsimd.memset(self.magic[:], MAGIC).then_inc(step, 1)
        rounder = self.magic[:].unsqueeze(2).to_broadcast((P, HEADS, HD))
        pool.wait_ge(self.scaled, 5)
        for t in range(T):
            nc.gpsimd.tensor_tensor(heads_of(q[:, t, :]), heads_of(q[:, t, :]), per_head(self.inv[:, t, :]),
                                    ALU.mult).then_inc(step, 1)
        pool.wait_ge(step, 1 + T)
        for t in range(T):
            nc.gpsimd.tensor_tensor(heads_of(q[:, t, :]), heads_of(q[:, t, :]), rounder, ALU.add).then_inc(step, 1)
        pool.wait_ge(step, 1 + 2 * T)
        for t in range(T):
            for c in range(2):
                nc.gpsimd.tensor_tensor(self.twice[:, t, :, c, :], heads_of(q[:, t, :]), rounder,
                                        ALU.subtract).then_inc(step, 1)
        pool.wait_ge(step, 1 + 4 * T)


def keys_and_values(chip, ctx_d, rows, rows_loaded, w_hi, w_lo, bias, kt_d, v_d, vmax, ident32, ident16, queries):
    nc = chip.nc
    NC = 2 * D // HALF
    vmax_cleared = chip.sem("kv_vmax_cleared")
    with ExitStack() as ctx:
        xt_hi = [chip.sb(ctx, f"kv_xthi{s}", [P, KD, P], F16) for s in range(2)]
        xt_lo = [chip.sb(ctx, f"kv_xtlo{s}", [P, KD, P], F16) for s in range(2)]
        key = [chip.sb(ctx, f"kv_key{s}", [P, D], F32) for s in range(2)]
        amax, scale, inv, scale64 = (chip.sb(ctx, f"kv_{n}", [P, HEADS], F32) for n in ("amax", "scale", "inv", "sc64"))
        parts = [chip.sb(ctx, f"kv_parts{s}", [P, HEADS, 2, HD], F16) for s in range(2)]
        kt = chip.sb(ctx, "kv_kt", [P, HEADS, 2 * P], F16)
        val = chip.sb(ctx, "kv_val", [P, HEADS, 2, HD], F32)
        vabs = chip.sb(ctx, "kv_vabs", [P, D], F32)
        acc = [chip.ps(ctx, f"kv_acc{c}", [P, HALF], F32) for c in range(NC)]
        turn = chip.ps(ctx, "kv_turn", [P, KD, P], F32)
        kturn = chip.ps(ctx, "kv_kturn", [P, HEADS, P], F16)
        rows_turned = chip.sem("kv_rows_turned")
        hi_ready, lo_ready = chip.sem("kv_xt_hi"), chip.sem("kv_xt_lo")
        summed, taken = chip.sem("kv_summed"), chip.sem("kv_taken")
        step, int_ready = chip.sem("kv_steps"), chip.sem("kv_int_ready")
        khi_ready, parts_ready = chip.sem("kv_khi"), chip.sem("kv_parts_ready")
        keys_turned, kt_ready = chip.sem("kv_keys_turned"), chip.sem("kv_kt_ready")
        abs_ready = chip.sem("kv_abs")
        kt_stored, v_stored, v_ready = chip.sem("kv_kt_stored"), chip.sem("kv_v_stored"), chip.sem("kv_v_ready")
        block = ctx.enter_context(nc.Block())
        LAST_PAIR = KVT // 2 - 1
        STEPS = 6

        def each_pair(eng, body):
            body(0, True, False)
            with eng.Fori(1, LAST_PAIR) as i:
                body(i, False, False)
            body(LAST_PAIR, False, True)

        @block.sync
        def _(sp):
            def load(row, s):
                sp.dma_start(rows[s][:], row).then_inc(rows_loaded[s], 16)

            def store_keys(i):
                dst = kt_d[:, :, bass.ds(i * (2 * P), 2 * P)].rearrange("h p n -> p h n")
                sp.dma_start(dst, kt[:]).then_inc(kt_stored, 16)

            def body(i, first, last):
                if not first:
                    sp.wait_ge(kt_ready, 2 * i)
                    store_keys(i - 1)
                if not last:
                    for s in range(2):
                        sp.wait_ge(rows_turned, 2 * i + s + 1)
                        load(ctx_d[bass.ds(2 * i + 2 + s, 1)].rearrange("a p n -> (a p) n"), s)
                sp.wait_ge(v_ready, 2 * i + 2)
                dst = v_d[:, :, bass.ds(2 * i, 2), :].rearrange("h p a d -> p h a d")
                sp.dma_start(dst, val[:]).then_inc(v_stored, 16)

            each_pair(sp, body)
            sp.wait_ge(kt_ready, KVT)
            store_keys(LAST_PAIR)

        @block.tensor
        def _(pe):
            def turn_rows(i, s):
                pe.wait_ge(rows_loaded[s], 16 * i + 16)
                for k in range(KD):
                    last = nc.tensor.transpose(turn[:, k, :], rows[s][:, k * P:(k + 1) * P], ident32[:])
                last.then_inc(rows_turned, 1)

            def turn_keys(u, s):
                pe.wait_ge(parts_ready, u + 1)
                for h in range(HEADS):
                    last = nc.tensor.transpose(kturn[:, h, :], parts[s][:, h].rearrange("p c d -> p (c d)"), ident16[:])
                last.then_inc(keys_turned, 1)

            def products(u, s, c):
                for k in range(KD):
                    for q, (a, b) in enumerate(((xt_hi, w_hi), (xt_hi, w_lo), (xt_lo, w_hi))):
                        last = nc.tensor.matmul(acc[c][:], a[s][:, k, :], b[:, c, k, :],
                                                start=(k == 0 and q == 0), stop=(k == KD - 1 and q == 2))
                last.then_inc(summed, 1)

            def body(i, first, last):
                for s in range(2):
                    u = 2 * i + s
                    pe.wait_ge(lo_ready, u + 1)
                    for c in range(NC):
                        if not (first and s == 0):
                            pe.wait_ge(taken, NC * (u - 1) + c + 1)
                        products(u, s, c)
                        if c == 0 and not (last and s == 1):
                            turn_rows(i + s, 1 - s)
                        if c == 1 and not (first and s == 0):
                            if not (first and s == 1):
                                pe.wait_ge(kt_ready, u - 1)
                            turn_keys(u - 1, 1 - s)

            turn_rows(0, 0)
            each_pair(pe, body)
            pe.wait_ge(kt_ready, KVT - 1)
            turn_keys(KVT - 1, 1)

        @block.scalar
        def _(act):
            def rows_high(u, s):
                act.wait_ge(rows_turned, u + 1)
                nc.scalar.activation(xt_hi[s][:], turn[:], ACT.Copy, scale=X_SCALE).then_inc(hi_ready, 1)

            def keys_out(u, s, wait_store, i):
                act.wait_ge(keys_turned, u + 1)
                if wait_store:
                    act.wait_ge(kt_stored, 16 * i)
                nc.scalar.activation(kt[:, :, s * P:(s + 1) * P], kturn[:], ACT.Copy).then_inc(kt_ready, 1)

            def body(i, first, last):
                for s in range(2):
                    u = 2 * i + s
                    if not (last and s == 1):
                        rows_high(u + 1, 1 - s)
                    if not (first and s == 0):
                        keys_out(u - 1, 1 - s, s == 1 and not first, i)
                    act.wait_ge(int_ready, u + 1)
                    nc.scalar.activation(parts[s][:, :, 0, :], heads_of(key[s][:]), ACT.Copy).then_inc(khi_ready, 1)
                    act.wait_ge(taken, NC * (u + 1))
                    if not (first and s == 0):
                        act.wait_ge(v_ready, u)
                    nc.scalar.activation(heads_of(vabs[:]), val[:, :, s, :], ACT.Abs).then_inc(abs_ready, 1)

            rows_high(0, 0)
            each_pair(act, body)
            keys_out(KVT - 1, 1, False, None)

        @block.vector
        def _(dve):
            def rows_low(u, s):
                dve.wait_ge(hi_ready, u + 1)
                nc.vector.scalar_tensor_tensor(out=xt_lo[s][:], in0=turn[:], scalar=X_SCALE, in1=xt_hi[s][:],
                                               op0=ALU.mult, op1=ALU.subtract).then_inc(lo_ready, 1)

            def key_chunk(u, s, c):
                dve.wait_ge(summed, NC * u + c + 1)
                cols = slice(c * HALF, (c + 1) * HALF)
                nc.vector.scalar_tensor_tensor(out=key[s][:, cols], in0=acc[c][:], scalar=UNSCALE,
                                               in1=bias[:, cols], op0=ALU.mult, op1=ALU.add).then_inc(taken, 1)

            def quantise(u, s):
                n = STEPS * u
                dve.wait_ge(taken, NC * u + 2)
                nc.vector.tensor_reduce(amax[:], heads_of(key[s][:]), AX.X, ALU.max,
                                        apply_absolute_value=True).then_inc(step, 1)
                dve.wait_ge(step, n + 1)
                nc.vector.tensor_scalar(scale[:], amax[:], 1.0 / LEVELS, 1e-8, ALU.mult, ALU.max).then_inc(step, 1)
                dve.wait_ge(step, n + 2)
                nc.vector.reciprocal(inv[:], scale[:]).then_inc(step, 1)
                nc.vector.tensor_scalar(scale64[:], scale[:], K_SCALE, None, ALU.mult).then_inc(step, 1)
                dve.wait_ge(step, n + 4)
                nc.vector.tensor_tensor(heads_of(key[s][:]), heads_of(key[s][:]), per_head(inv[:]),
                                        ALU.mult).then_inc(step, 1)
                dve.wait_ge(step, n + 5)
                nc.vector.tensor_scalar(key[s][:], key[s][:], MAGIC, MAGIC, ALU.add, ALU.subtract).then_inc(step, 1)
                dve.wait_ge(step, n + 6)
                nc.vector.tensor_tensor(heads_of(key[s][:]), heads_of(key[s][:]), per_head(scale64[:]),
                                        ALU.mult).then_inc(int_ready, 1)

            def low_parts(u, s):
                dve.wait_ge(khi_ready, u + 1)
                nc.vector.tensor_tensor(parts[s][:, :, 1, :], heads_of(key[s][:]), parts[s][:, :, 0, :],
                                        ALU.subtract).then_inc(parts_ready, 1)

            def value_chunk(u, s, c):
                dve.wait_ge(summed, NC * u + c + 1)
                cols = slice(c * HALF, (c + 1) * HALF)
                h = (c - 2) * (HALF // HD)
                nc.vector.scalar_tensor_tensor(
                    out=val[:, h:h + HALF // HD, s, :], in0=acc[c][:].rearrange("p (h d) -> p h d", d=HD),
                    scalar=UNSCALE, in1=bias[:, cols].rearrange("p (h d) -> p h d", d=HD),
                    op0=ALU.mult, op1=ALU.add).then_inc(taken, 1)

            def value_max(u, s, start):
                if not start:
                    dve.wait_ge(v_ready, u)
                dve.wait_ge(abs_ready, u + 1)
                nc.vector.tensor_tensor(vmax, vabs[:], vmax, ALU.max).then_inc(v_ready, 1)

            def body(i, first, last):
                for s in range(2):
                    u = 2 * i + s
                    key_chunk(u, s, 0)
                    if not (last and s == 1):
                        rows_low(u + 1, 1 - s)
                    key_chunk(u, s, 1)
                    quantise(u, s)
                    if s == 0 and not first:
                        dve.wait_ge(v_stored, 16 * i)
                    value_chunk(u, s, 2)
                    low_parts(u, s)
                    value_chunk(u, s, 3)
                    value_max(u, s, first and s == 0)

            nc.vector.memset(vmax, 0.0).then_inc(vmax_cleared, 1)
            dve.wait_ge(vmax_cleared, 1)
            rows_low(0, 0)
            queries.vector(dve)
            each_pair(dve, body)
            dve.wait_ge(v_ready, KVT)

        @block.gpsimd
        def _(pool):
            queries.gpsimd(pool)
    return (kt_stored, 16 * (LAST_PAIR + 1)), (v_stored, 16 * (LAST_PAIR + 1))


class HeadLoads:

    def __init__(self, chip, ctx, kt_d, v_d):
        self.kt_d, self.v_d = kt_d, v_d
        self.kt = [chip.sb(ctx, f"at_kt{j}", [P, NKV], F16) for j in range(2)]
        self.v_raw = chip.sb(ctx, "at_v_raw", [P, KVT, HD], F32)
        self.scales_loaded = chip.sem("at_scales_loaded")
        self.kt_loaded, self.v_loaded = [chip.sem(f"at_kt_loaded{j}") for j in range(2)], chip.sem("at_v_loaded")

    def keys(self, sp, head, j):
        sp.dma_start(self.kt[j][:], self.kt_d[bass.ds(head, 1)].rearrange("a p n -> (a p) n"))\
            .then_inc(self.kt_loaded[j], 16)

    def values(self, sp, head):
        sp.dma_start(self.v_raw[:], self.v_d[bass.ds(head, 1)].rearrange("a p n d -> (a p) n d"))\
            .then_inc(self.v_loaded, 16)


def value_scales(chip, vmax, scale_d, v_scale, twice, q_t, ident32, ident16, stores, heads):
    nc = chip.nc
    turned, reduced, out, step = (chip.sem(f"vs_{n}") for n in ("turned", "reduced", "out", "steps"))
    with ExitStack() as ctx:
        col = chip.sb(ctx, "vs_col", [P, 2, KD], F32)
        bank = chip.ps(ctx, "vs_turn", [P, KD, P], F32)
        q_bank = [chip.ps(ctx, f"qq_turn{n}", [P, 8, P], F16) for n in range(4)]
        q_turned, q_t_ready = chip.sem("qq_turned"), chip.sem("qq_t_ready")
        units = [(t, g) for t in range(T) for g in range(2)]
        block = ctx.enter_context(nc.Block())

        @block.tensor
        def _(pe):
            for k in range(KD):
                last = nc.tensor.transpose(bank[:, k, :], vmax[:, k * P:(k + 1) * P], ident32[:])
            last.then_inc(turned, 1)
            for n, (t, g) in enumerate(units):
                if n >= 4:
                    pe.wait_ge(q_t_ready, n - 3)
                for h in range(8):
                    last = nc.tensor.transpose(q_bank[n % 4][:, h, :],
                                               twice[:, t, 8 * g + h, :, :].rearrange("p c d -> p (c d)"), ident16[:])
                last.then_inc(q_turned, 1)

        @block.vector
        def _(dve):
            dve.wait_ge(turned, 1)
            nc.vector.tensor_reduce(col[:, 0, :], bank[:], AX.X, ALU.max).then_inc(step, 1)
            dve.wait_ge(step, 1)
            nc.vector.tensor_scalar(col[:, 0, :], col[:, 0, :], 1.0 / LEVELS, 1e-8, ALU.mult, ALU.max)\
                .then_inc(step, 1)
            dve.wait_ge(step, 2)
            nc.vector.reciprocal(col[:, 1, :], col[:, 0, :]).then_inc(reduced, 1)
            for n, (t, g) in enumerate(units):
                dve.wait_ge(q_turned, n + 1)
                nc.vector.tensor_copy(q_t[:, 8 * g:8 * g + 8, t * P:(t + 1) * P], q_bank[n % 4][:])\
                    .then_inc(q_t_ready, 1)
            dve.wait_ge(q_t_ready, len(units))

        @block.sync
        def _(sp):
            sp.wait_ge(reduced, 1)
            sp.dma_start(scale_d.rearrange("(c k p) -> p (c k)", p=P, c=2), col[:].rearrange("p c k -> p (c k)"),
                         allow_slow_non_contiguous=True).then_inc(out, 16)
            for stored, count in stores:
                sp.wait_ge(stored, count)
            sp.wait_ge(out, 16)
            sp.dma_start(v_scale[:].rearrange("p c n -> p (c n)"), flat_bcast(scale_d, 2 * D))\
                .then_inc(heads.scales_loaded, 16)
            heads.values(sp, 0)
            heads.keys(sp, 0, 0)
            heads.keys(sp, 1, 1)


def attend_quantised(chip, q_t, exp_scale, heads, v_scale, twice, o, ident16):
    nc = chip.nc
    SLOTS = 2 * T
    SC = 1024
    CH = NKV // SC
    GB = SC // P
    EC = 2048
    NE = NKV // EC
    PAIRS = HEADS // 2
    AHEAD = 2
    LN_TOP = float(np.log(255.0))
    kt, v_raw, kt_loaded, v_loaded = heads.kt, heads.v_raw, heads.kt_loaded, heads.v_loaded
    q_ready, v_quantised = chip.sem("at_q_ready"), chip.sem("at_v_quant")
    v_step, filled, copied = chip.sem("at_v_steps"), chip.sem("at_filled"), chip.sem("at_copied")
    bias_ready, bias_step, exp_done = chip.sem("at_bias_ready"), chip.sem("at_bias_steps"), chip.sem("at_exp")
    turned, summed = chip.sem("at_turned"), chip.sem("at_summed")
    magic_set = chip.sem("at_magic_set")
    out_even, out_odd = chip.sem("at_out_even"), chip.sem("at_out_odd")
    inv_step, o_taken, o_moved = chip.sem("at_inv_steps"), chip.sem("at_o_taken"), chip.sem("at_o_moved")
    COPIED0, EXP0, TURNED0, BANK0, SUMMED0, TAKEN0, MOVED0 = 2, 2 * NE, 4, 1, 4, 2, 2
    with ExitStack() as ctx:
        magic = chip.sb(ctx, "at_magic", [P, 1], F32)
        v_room = twice[:].rearrange("p t h c d -> p (t h c d)").rearrange("p (j k d) -> p j k d", j=2, d=HD)
        v_int = [v_room[:, j] for j in range(2)]
        sc = [chip.sb(ctx, f"at_sc{j}", [P, NKV], F32) for j in range(2)]
        prob = [chip.sb(ctx, f"at_prob{j}", [P, EC], U16) for j in range(2)]
        probt = [chip.sb(ctx, f"at_probt{j}", [P, GB, P], F16) for j in range(4)]
        q_pair = [chip.sb(ctx, f"at_q{j}", [P, T * P], F16) for j in range(2)]
        qs_pair = [chip.sb(ctx, f"at_qs{j}", [P, T], F32) for j in range(2)]
        vs_pair = [chip.sb(ctx, f"at_vs{j}", [P, HD], F32) for j in range(2)]
        vi_head = chip.sb(ctx, "at_vi", [P, HD], F32)
        o_pair = [chip.sb(ctx, f"at_o{j}", [P, T, HD], F32) for j in range(2)]
        part_max = [chip.sb(ctx, f"at_pmax{j}", [P, CH], F32) for j in range(2)]
        neg_max = [chip.sb(ctx, f"at_nmax{j}", [P, 1], F32) for j in range(2)]
        bias = [chip.sb(ctx, f"at_bias{j}", [P, 1], F32) for j in range(2)]
        part_sum = [chip.sb(ctx, f"at_psum{j}", [P, NE], F32) for j in range(2)]
        total = [chip.sb(ctx, f"at_total{j}", [P, 1], F32) for j in range(2)]
        inv = [chip.sb(ctx, f"at_inv{j}", [P, 1], F32) for j in range(2)]
        score = [chip.ps(ctx, f"at_score{j}", [P, SC], F32) for j in range(2)]
        turn = [chip.ps(ctx, f"at_turn{j}", [P, GB, P], F16) for j in range(2)]
        outp = [chip.ps(ctx, f"at_outp{j}", [P, HALF], F32) for j in range(2)]
        block = ctx.enter_context(nc.Block())

        def each_pair(eng, body):
            body(0, True, False)
            with eng.Fori(1, PAIRS - 1) as i:
                body(i, False, False)
            body(PAIRS - 1, False, True)

        @block.sync
        def _(sp):
            sp.wait_ge(v_quantised, 1)
            heads.values(sp, 1)
            with sp.Fori(0, PAIRS - 1) as i:
                for j in range(2):
                    sp.wait_ge(filled, CH * (i * SLOTS + T * (j + 1)))
                    heads.keys(sp, 2 * i + 2 + j, j)
                    sp.wait_ge(v_quantised, 2 * i + 2 + j)
                    heads.values(sp, 2 * i + 2 + j)
            sp.wait_ge(v_loaded, 16 * HEADS)

        @block.gpsimd
        def _(pool):
            pool.sem_inc(o_moved, MOVED0)
            rounder = magic[:].unsqueeze(2).to_broadcast((P, KVT, HD))
            nc.gpsimd.memset(magic[:], MAGIC).then_inc(magic_set, 1)
            pool.wait_ge(magic_set, 1)
            pool.wait_ge(heads.scales_loaded, 16)

            def fetch(head, j):
                nc.gpsimd.tensor_copy(q_pair[j][:], q_t[:, bass.ds(head, 1), :].rearrange("p a n -> p (a n)"))\
                    .then_inc(q_ready, 1)
                nc.gpsimd.tensor_copy(qs_pair[j][:], exp_scale[:, bass.ds(head, 1), :].rearrange("p a n -> p (a n)"))\
                    .then_inc(q_ready, 1)
                nc.gpsimd.tensor_copy(vs_pair[j][:], v_scale[:, 0, bass.ds(head * HD, HD)]).then_inc(v_step, 1)
                nc.gpsimd.tensor_copy(vi_head[:], v_scale[:, 1, bass.ds(head * HD, HD)]).then_inc(v_step, 1)
                pool.wait_ge(v_step, 4 * head + 2)
                pool.wait_ge(v_loaded, 16 * head + 16)
                nc.gpsimd.tensor_tensor(v_raw[:], v_raw[:], vi_head[:].unsqueeze(1).to_broadcast((P, KVT, HD)),
                                        ALU.mult).then_inc(v_step, 1)
                pool.wait_ge(v_step, 4 * head + 3)
                nc.gpsimd.tensor_tensor(v_raw[:], v_raw[:], rounder, ALU.add).then_inc(v_step, 1)
                pool.wait_ge(v_step, 4 * head + 4)
                nc.gpsimd.tensor_tensor(v_int[j], v_raw[:], rounder, ALU.subtract).then_inc(v_quantised, 1)

            def move_out(i, j):
                head = 2 * i + j
                pool.wait_ge(o_taken, TAKEN0 + i * SLOTS + T * (j + 1))
                nc.gpsimd.tensor_copy(o[:, :, bass.ds(head * HD, HD)], o_pair[j][:]).then_inc(o_moved, 1)

            fetch(0, 0)
            fetch(1, 1)

            def body(i, first, last):
                for j in range(2):
                    move_out(i, j)
                    if not last:
                        fetch(2 * i + 2 + j, j)

            each_pair(pool, body)
            pool.wait_ge(o_moved, MOVED0 + HEADS)

        @block.tensor
        def _(pe):
            pe.sem_inc(turned, TURNED0)
            pe.sem_inc(summed, SUMMED0)

            def scores(g, n, c):
                n = n % SLOTS
                j, t = n // T, n % T
                pe.wait_ge(copied, g * CH + c - 1 + COPIED0)
                for b in range(SC // HALF):
                    cols = slice(c * SC + b * HALF, c * SC + (b + 1) * HALF)
                    last = nc.tensor.matmul(score[c % 2][:, b * HALF:(b + 1) * HALF], q_pair[j][:, t * P:(t + 1) * P],
                                            kt[j][:, cols], start=True, stop=True)
                last.then_inc(filled, 1)

            def turns(g, c):
                if c % 2 == 0:
                    pe.wait_ge(exp_done, EXP0 + g * NE + c // 2 + 1)
                    pe.wait_ge(out_even, BANK0 + g * (CH // 2) + c // 2)
                else:
                    pe.wait_ge(out_odd, BANK0 + g * (CH // 2) + c // 2)
                for b in range(GB):
                    at = (c % 2) * SC + b * P
                    last = nc.tensor.transpose(turn[c % 2][:, b, :], prob[(c // 2) % 2][:, at:at + P].bitcast(F16),
                                               ident16[:])
                last.then_inc(turned, 1)

            def sums(g, n, c):
                if c == 0:
                    pe.wait_ge(o_taken, g + 1 - 2 + TAKEN0)
                pe.wait_ge((out_even, out_odd)[c % 2], BANK0 + g * (CH // 2) + c // 2 + 1)
                for b in range(GB):
                    last = nc.tensor.matmul(outp[n % 2][:, 0:HD], probt[c % 4][:, b, :], v_int[n // T][:, c * GB + b, :],
                                            start=(c == 0 and b == 0), stop=(c == CH - 1 and b == GB - 1))
                last.then_inc(summed, 1)

            def inputs_ready(i, n):
                if n % T == 0:
                    k, j = n // SLOTS, (n % SLOTS) // T
                    pe.wait_ge(kt_loaded[j], (i + k) * 16 + 16)
                    pe.wait_ge(q_ready, 4 * (i + k) + 2 * j + 2)

            def body(i, first, last):
                for n in range(SLOTS):
                    g = i * SLOTS + n
                    for c in range(CH):
                        ahead, cc = (n + 1, c + AHEAD) if c + AHEAD < CH else (n + 2, c + AHEAD - CH)
                        if not (last and ahead >= SLOTS):
                            if cc == 0:
                                inputs_ready(i, ahead)
                            scores(i * SLOTS + ahead, ahead, cc)
                        if c % 2 == 1:
                            turns(g, c - 1)
                            turns(g, c)
                            if c == 3 and n % T == 0:
                                pe.wait_ge(v_quantised, 2 * i + n // T + 1)
                            if c >= 3:
                                sums(g, n, c - 3)
                                sums(g, n, c - 2)
                            elif not (first and n == 0):
                                sums(g - 1, (n - 1) % SLOTS, CH - 2)
                                sums(g - 1, (n - 1) % SLOTS, CH - 1)

            inputs_ready(0, 0)
            for c in range(CH + AHEAD):
                scores(c // CH, c // CH, c % CH)
            each_pair(pe, body)
            sums(HEADS * T - 1, SLOTS - 1, CH - 2)
            sums(HEADS * T - 1, SLOTS - 1, CH - 1)

        @block.vector
        def _(dve):
            dve.sem_inc(copied, COPIED0)
            dve.sem_inc(out_even, BANK0)
            dve.sem_inc(o_taken, TAKEN0)

            def copy(g, n, c):
                if c == 0:
                    dve.wait_ge(exp_done, (g - 1) * NE + EXP0)
                dve.wait_ge(filled, g * CH + c + 1)
                nc.vector.tensor_scalar(sc[n % 2][:, c * SC:(c + 1) * SC], score[c % 2][:], 1.0, None, ALU.mult, ALU.max,
                                        accum_out=part_max[n % 2][:, c:c + 1]).then_inc(copied, 1)

            def find_max(g, n):
                dve.wait_ge(copied, COPIED0 + (g + 1) * CH)
                nc.vector.tensor_reduce(neg_max[n % 2][:], part_max[n % 2][:], AX.X, ALU.max, negate=True)\
                    .then_inc(bias_step, 1)

            def make_bias(g, n):
                dve.wait_ge(bias_step, g + 1)
                j, t = (n % SLOTS) // T, n % T
                nc.vector.tensor_scalar(bias[n % 2][:], neg_max[n % 2][:], qs_pair[j][:, t:t + 1], LN_TOP,
                                        ALU.mult, ALU.add).then_inc(bias_ready, 1)

            def turned_out(g, c):
                dve.wait_ge(turned, TURNED0 + g * CH + c + 1)
                dve.wait_ge(summed, g * CH + c + 1 - 4 + SUMMED0)
                nc.vector.tensor_copy(probt[c % 4][:], turn[c % 2][:].bitcast(U16)).then_inc(out_even, 1)

            def total_sum(g, n):
                dve.wait_ge(summed, SUMMED0 + (g + 1) * CH)
                nc.vector.tensor_reduce(total[n % 2][:], part_sum[n % 2][:], AX.X, ALU.add).then_inc(inv_step, 1)

            def inverse(g, n):
                dve.wait_ge(inv_step, 2 * g + 1)
                nc.vector.reciprocal(inv[n % 2][:], total[n % 2][:]).then_inc(inv_step, 1)

            def output(i, g, n):
                dve.wait_ge(inv_step, 2 * g + 2)
                j, t = n // T, n % T
                if t == 0:
                    dve.wait_ge(o_moved, 2 * i + j + 1 - 2 + MOVED0)
                nc.vector.scalar_tensor_tensor(out=o_pair[j][:, t, :], in0=outp[n % 2][:, 0:HD], scalar=inv[n % 2][:],
                                               in1=vs_pair[j][:], op0=ALU.mult, op1=ALU.mult).then_inc(o_taken, 1)

            def body(i, first, last):
                for n in range(SLOTS):
                    g = i * SLOTS + n
                    for c in range(CH):
                        ahead, cc = (n + 1, c + AHEAD) if c + AHEAD < CH else (n + 2, c + AHEAD - CH)
                        if not (last and ahead >= SLOTS):
                            copy(i * SLOTS + ahead, ahead, cc)
                        biased = c + AHEAD == CH - 1 and not (last and ahead >= SLOTS)
                        before = not (first and n == 0)
                        if biased:
                            find_max(i * SLOTS + ahead, ahead)
                        if c == 3 and before:
                            total_sum(g - 1, (n - 1) % SLOTS)
                        if c == 4 and before:
                            output(i if n else i - 1, g - 1, (n - 1) % SLOTS)
                        if c % 2 == 1:
                            turned_out(g, c - 1)
                        if biased:
                            make_bias(i * SLOTS + ahead, ahead)
                        if c == 3 and before:
                            inverse(g - 1, (n - 1) % SLOTS)

            for c in range(CH + AHEAD):
                copy(c // CH, c // CH, c % CH)
                if c == CH - 1:
                    dve.wait_ge(q_ready, 2)
                    find_max(0, 0)
                    make_bias(0, 0)
            each_pair(dve, body)
            total_sum(HEADS * T - 1, SLOTS - 1)
            inverse(HEADS * T - 1, SLOTS - 1)
            output(PAIRS - 1, HEADS * T - 1, SLOTS - 1)
            dve.wait_ge(o_taken, TAKEN0 + HEADS * T)

        @block.scalar
        def _(act):
            act.sem_inc(exp_done, EXP0)
            act.sem_inc(out_odd, BANK0)

            def exps(g, n, e):
                if e == 0:
                    act.wait_ge(bias_ready, g + 1)
                    act.wait_ge(o_taken, g + 1 - 2 + TAKEN0)
                act.wait_ge(turned, (g * NE + e - 2) * 2 + 2 + TURNED0)
                j, t = n // T, n % T
                nc.scalar.activation(prob[e % 2][:], sc[n % 2][:, e * EC:(e + 1) * EC], ACT.Exp, bias=bias[n % 2][:],
                                     scale=qs_pair[j][:, t:t + 1], accum_out=part_sum[n % 2][:, e:e + 1])\
                    .then_inc(exp_done, 1)

            def turned_out(g, c):
                act.wait_ge(turned, TURNED0 + g * CH + c + 1)
                act.wait_ge(summed, g * CH + c + 1 - 4 + SUMMED0)
                nc.scalar.activation(probt[c % 4][:], turn[c % 2][:].bitcast(U16), ACT.Copy).then_inc(out_odd, 1)

            def body(i, first, last):
                for n in range(SLOTS):
                    g = i * SLOTS + n
                    exps(g, n, 0)
                    if not (first and n == 0):
                        turned_out(g - 1, CH - 1)
                    for e in range(1, NE):
                        exps(g, n, e)
                        turned_out(g, 2 * e - 1)

            each_pair(act, body)
            turned_out(HEADS * T - 1, CH - 1)
            act.wait_ge(out_odd, BANK0 + HEADS * T * CH // 2)


def rotate(nc, pool, y, step, n, cos, sin, swapped):
    for t in range(T):
        rows = heads_of(y[:, t, :])
        pairs, out = (a.rearrange("p r (i e) -> p r i e", e=2) for a in (rows, swapped[:, t]))
        table = sin.rearrange("p (i e) -> p i e", e=2)
        for e in range(2):
            nc.gpsimd.tensor_tensor(out[:, :, :, e], pairs[:, :, :, 1 - e],
                                    table[:, :, e].unsqueeze(1).to_broadcast((P, HEADS, HD // 2)),
                                    ALU.mult).then_inc(step, 1)
    pool.wait_ge(step, n + 2 * T)
    for t in range(T):
        rows = heads_of(y[:, t, :])
        nc.gpsimd.tensor_tensor(rows, rows, cos.unsqueeze(1).to_broadcast((P, HEADS, HD)),
                                ALU.mult).then_inc(step, 1)
    pool.wait_ge(step, n + 3 * T)
    for t in range(T):
        rows = heads_of(y[:, t, :])
        nc.gpsimd.tensor_tensor(rows, rows, swapped[:, t], ALU.add).then_inc(step, 1)
    pool.wait_ge(step, n + 4 * T)
    return n + 4 * T


def attend_causal(chip, y_q, y_k, y_v, mask, o, ident32):
    nc = chip.nc
    turned, q_out, k_out = chip.sem("ca_turned"), chip.sem("ca_q_out"), chip.sem("ca_k_out")
    scored, masked, maxed = chip.sem("ca_scored"), chip.sem("ca_masked"), chip.sem("ca_maxed")
    exps_done, p_turned, p_out = chip.sem("ca_exp"), chip.sem("ca_p_turned"), chip.sem("ca_p_out")
    summed, inv_ready, o_ready = chip.sem("ca_summed"), chip.sem("ca_inv"), chip.sem("ca_o")
    HG = 4
    groups = [(t, c) for t in range(T) for c in range(HEADS // HG)]
    G = len(groups)

    def head_of(c, j):
        return 2 * HG * (c // 2) + 2 * j + c % 2

    with ExitStack() as ctx:
        q_t = chip.sb(ctx, "ca_qt", [P, KD, T * P], F32)
        k_t = chip.sb(ctx, "ca_kt", [P, KD, T * P], F32)
        s = [chip.sb(ctx, f"ca_s{j}", [P, HG, P], F32) for j in range(2)]
        p_t = [chip.sb(ctx, f"ca_pt{j}", [P, HG, P], F32) for j in range(2)]
        neg_max = [chip.sb(ctx, f"ca_nm{j}", [P, HG], F32) for j in range(2)]
        total = [chip.sb(ctx, f"ca_tot{j}", [P, HG], F32) for j in range(2)]
        inv = [chip.sb(ctx, f"ca_inv{j}", [P, HG], F32) for j in range(2)]
        with ExitStack() as tctx:
            bq = [chip.ps(tctx, f"ca_bq{n}", [P, 4, P], F32) for n in range(2)]
            bk = [chip.ps(tctx, f"ca_bk{n}", [P, 4, P], F32) for n in range(2)]
            block = tctx.enter_context(nc.Block())
            units = [(t, h) for t in range(T) for h in range(2)]

            @block.tensor
            def _(pe):
                for n, (t, h) in enumerate(units):
                    if n >= 2:
                        pe.wait_ge(q_out, n - 1)
                        pe.wait_ge(k_out, n - 1)
                    for y, bank in ((y_q, bq), (y_k, bk)):
                        for k in range(4):
                            at = (4 * h + k) * P
                            last = nc.tensor.transpose(bank[n % 2][:, k, :], y[:, t, at:at + P], ident32[:])
                    last.then_inc(turned, 1)

            @block.scalar
            def _(act):
                for n, (t, h) in enumerate(units):
                    act.wait_ge(turned, n + 1)
                    nc.scalar.activation(q_t[:, 4 * h:4 * h + 4, t * P:(t + 1) * P], bq[n % 2][:], ACT.Copy)\
                        .then_inc(q_out, 1)

            @block.vector
            def _(dve):
                for n, (t, h) in enumerate(units):
                    dve.wait_ge(turned, n + 1)
                    nc.vector.tensor_copy(k_t[:, 4 * h:4 * h + 4, t * P:(t + 1) * P], bk[n % 2][:])\
                        .then_inc(k_out, 1)
                dve.wait_ge(k_out, len(units))

        score = [chip.ps(ctx, f"ca_score{n}", [P, HG, P], F32) for n in range(2)]
        turn = [chip.ps(ctx, f"ca_turn{n}", [P, HG, P], F32) for n in range(2)]
        outp = [chip.ps(ctx, f"ca_outp{n}", [P, HG, P], F32) for n in range(2)]
        block = ctx.enter_context(nc.Block())

        @block.tensor
        def _(pe):
            def scores(g):
                t, c = groups[g]
                if g >= 2:
                    pe.wait_ge(masked, g - 1)
                for j in range(HG):
                    h = head_of(c, j)
                    rows, tok = slice(HD * (h % 2), HD * (h % 2) + HD), slice(t * P, (t + 1) * P)
                    last = nc.tensor.matmul(score[g % 2][:, j, :], q_t[rows, h // 2, tok], k_t[rows, h // 2, tok],
                                            start=True, stop=True)
                last.then_inc(scored, 1)

            def turns(g):
                pe.wait_ge(exps_done, HG * (g + 1))
                if g >= 2:
                    pe.wait_ge(p_out, g - 1)
                for j in range(HG):
                    last = nc.tensor.transpose(turn[g % 2][:, j, :], s[g % 2][:, j, :], ident32[:])
                last.then_inc(p_turned, 1)

            def sums(g):
                t, c = groups[g]
                pe.wait_ge(p_out, g + 1)
                if g >= 2:
                    pe.wait_ge(o_ready, g - 1)
                for j in range(HG):
                    h = head_of(c, j)
                    last = nc.tensor.matmul(outp[g % 2][:, j, 0:HD], p_t[g % 2][:, j, :], y_v[:, t, h * HD:(h + 1) * HD],
                                            start=True, stop=True)
                last.then_inc(summed, 1)

            scores(0)
            for g in range(G):
                if g + 1 < G:
                    scores(g + 1)
                turns(g)
                if g >= 1:
                    sums(g - 1)
            sums(G - 1)

        @block.vector
        def _(dve):
            def masks(g):
                dve.wait_ge(scored, g + 1)
                if g >= 2:
                    dve.wait_ge(p_turned, g - 1)
                nc.vector.scalar_tensor_tensor(out=s[g % 2][:], in0=score[g % 2][:], scalar=HD ** -0.5,
                                               in1=mask[:].unsqueeze(1).to_broadcast((P, HG, P)), op0=ALU.mult,
                                               op1=ALU.add).then_inc(masked, 1)
                dve.wait_ge(masked, g + 1)
                nc.vector.tensor_reduce(neg_max[g % 2][:], s[g % 2][:], AX.X, ALU.max, negate=True).then_inc(maxed, 1)

            def outputs(g):
                t, c = groups[g]
                dve.wait_ge(summed, g + 1)
                nc.vector.reciprocal(inv[g % 2][:], total[g % 2][:]).then_inc(inv_ready, 1)
                dve.wait_ge(inv_ready, g + 1)
                nc.vector.tensor_tensor(
                    o[:, t, :].rearrange("p (c h e d) -> p c h e d", h=HG, e=2, d=HD)[:, c // 2, :, c % 2, :],
                    outp[g % 2][:, :, 0:HD], inv[g % 2][:].unsqueeze(2).to_broadcast((P, HG, HD)),
                    ALU.mult).then_inc(o_ready, 1)

            masks(0)
            for g in range(G):
                if g + 1 < G:
                    masks(g + 1)
                if g >= 1:
                    outputs(g - 1)
            outputs(G - 1)
            dve.wait_ge(o_ready, G)

        @block.scalar
        def _(act):
            def exps(g):
                act.wait_ge(maxed, g + 1)
                if g >= 2:
                    act.wait_ge(inv_ready, g - 1)
                for j in range(HG):
                    nc.scalar.activation(s[g % 2][:, j, :], s[g % 2][:, j, :], ACT.Exp, bias=neg_max[g % 2][:, j:j + 1],
                                         accum_out=total[g % 2][:, j:j + 1]).then_inc(exps_done, 1)

            def turned_out(g):
                act.wait_ge(p_turned, g + 1)
                if g >= 2:
                    act.wait_ge(summed, g - 1)
                nc.scalar.activation(p_t[g % 2][:], turn[g % 2][:], ACT.Copy).then_inc(p_out, 1)

            exps(0)
            for g in range(G):
                if g + 1 < G:
                    exps(g + 1)
                turned_out(g)


MAGNITUDE, SIGN = 0x0E000E00, 0x80008000 - (1 << 32)


def shift_of(bits):
    return (ALU.logical_shift_left, bits) if bits >= 0 else (ALU.logical_shift_right, -bits)


class Unpacker:

    STEPS = 9

    def __init__(self, chip, ctx, tag, cols):
        self.nc, self.cols = chip.nc, cols
        self.mag = chip.sb(ctx, f"{tag}_mag", [P, 4, 2 * cols], I32)
        self.sign = chip.sb(ctx, f"{tag}_sign", [P, 4, 2 * cols], I32)
        self.packed = self.sign[:, 3, :]
        self.prod = [chip.sb(ctx, f"{tag}_prod{j}", [P, 4, cols, 2], F32) for j in range(2)]
        self.step, self.taken = chip.sem(f"{tag}_steps"), chip.sem(f"{tag}_taken")
        self.prod_ready = chip.sem(f"{tag}_prod_ready")
        self.hi_ready, self.lo_ready = chip.sem(f"{tag}_hi"), [chip.sem(f"{tag}_lo{g}") for g in range(2)]

    def products(self, dve, c, turned, blocks, scales):
        nc = self.nc
        if c:
            dve.wait_ge(self.step, self.STEPS * c)
        for g in range(2):
            dve.wait_ge(turned, 2 * c + g + 1)
            nc.vector.tensor_scalar(self.packed[:, g * self.cols:(g + 1) * self.cols], blocks[g], -1, None,
                                    ALU.bitwise_and).then_inc(self.taken, 1)
        if c:
            dve.wait_ge(self.prod_ready, 2 * c)
        dve.wait_ge(self.taken, 2 * c + 2)
        for k in range(4):
            op, by = shift_of(9 - 4 * k)
            nc.vector.tensor_scalar(self.mag[:, k, :], self.packed, by, MAGNITUDE, op, ALU.bitwise_and)\
                .then_inc(self.step, 1)
            op, by = shift_of(12 - 4 * k)
            if k == 3:
                dve.wait_ge(self.step, self.STEPS * c + 7)
            nc.vector.tensor_scalar(self.sign[:, k, :], self.packed, by, SIGN, op, ALU.bitwise_and)\
                .then_inc(self.step, 1)
        dve.wait_ge(self.step, self.STEPS * c + 8)
        nc.vector.tensor_tensor(self.mag[:], self.mag[:], self.sign[:], ALU.bitwise_or).then_inc(self.step, 1)
        dve.wait_ge(self.step, self.STEPS * c + 9)
        codes = self.mag[:].bitcast(F16).rearrange("p k (n e) -> p k n e", e=2)
        for g in range(2):
            if c:
                dve.wait_ge(self.lo_ready[g], c)
            nc.vector.tensor_tensor(self.prod[g][:], codes[:, :, g * self.cols:(g + 1) * self.cols, :],
                                    scales[g].unsqueeze(1).unsqueeze(3).to_broadcast((P, 4, self.cols, 2)),
                                    ALU.mult).then_inc(self.prod_ready, 1)

    @staticmethod
    def by_word(ap):
        return ap.rearrange("p (e k) n -> p k n e", e=2)

    def high(self, act, unit, j, dst):
        act.wait_ge(self.prod_ready, unit + 1)
        self.nc.scalar.activation(self.by_word(dst), self.prod[j][:], ACT.Copy).then_inc(self.hi_ready, 1)

    def low(self, eng, queue, c, g, dst_hi, dst):
        eng.wait_ge(self.hi_ready, 2 * c + g + 1)
        queue.tensor_tensor(self.by_word(dst), self.prod[g][:], self.by_word(dst_hi),
                            ALU.subtract).then_inc(self.lo_ready[g], 1)

    def wait(self, pe, c):
        for g in range(2):
            pe.wait_ge(self.lo_ready[g], c + 1)


def feed_forward(chip, turning, xt_hi, xt_lo, gu_d, gu_scale_d, dn_d, dn_scale_d, x, y, out_d, ident32):
    nc = chip.nc
    QC = 2
    NQ = WORD // QC
    COLS = QC * P
    NUP = NB * NQ
    down = [(half, b) for half in range(2) for b in range(NB)]
    UP_OUT = 1.0 / (X_SCALE * SC_SCALE * NIB_SCALE)
    DOWN_OUT = 1.0 / (H_SCALE * SC_SCALE * NIB_SCALE)
    SUMMED0, HID0, HLO0 = 2 * QC, QC, QC
    UP_SUMMED = SUMMED0 + QC * NUP
    with ExitStack() as ctx:
        w_hi = [chip.sb(ctx, f"ff_whi{j}", [P, WORD, 2 * COLS], F16) for j in range(2)]
        w_lo = [chip.sb(ctx, f"ff_wlo{j}", [P, WORD, 2 * COLS], F16) for j in range(2)]
        h_hi = chip.sb(ctx, "ff_hhi", [P, NB * WORD, T * P], F16)
        h_lo = chip.sb(ctx, "ff_hlo", [P, NB * WORD, T * P], F16)
        dn_scale = chip.sb(ctx, "ff_dn_scale", [P, NB, D], F16)
        dn_rows = chip.sb(ctx, "ff_dn_rows", [P, D // P, NB * P], I32)
        rows = [chip.sb(ctx, f"ff_rows{g}", [P, WORD, P], I32) for g in range(2)]
        raw = h_hi[:].rearrange("p k n -> p (k n)")[:, 0:2 * INNER]
        scale = chip.sb(ctx, "ff_scale", [P, 2 * NB, WORD, P], F16)
        sig = [chip.sb(ctx, f"ff_sig{j}", [P, T * P], F32) for j in range(2)]
        hid = [chip.sb(ctx, f"ff_hid{j}", [P, T * P], F32) for j in range(2)]
        small = chip.sb(ctx, "ff_small", [P, 5, T], F32)
        unpack = Unpacker(chip, ctx, "ff", COLS)
        sq = unpack.mag[:, 0:2, :].rearrange("p a n -> p (a n)").bitcast(F32)
        turn = [chip.ps(ctx, f"ff_turn{g}", [P, HALF], F32) for g in range(2)]
        turner = Turner(chip, ctx, [chip.ps(ctx, f"ff_xturn{g}", [P, HALF], F32) for g in range(2)], *turning)
        acc = [[chip.ps(ctx, f"ff_acc{j}{g}", [P, T * P], F32) for g in range(2)] for j in range(2)]
        dn_acc = acc[0] + acc[1]
        words = [t[:, 0:COLS].bitcast(I32) for t in turn]
        dn_cleared, dn_loaded, dn_scaled = chip.sem("ff_dn_cleared"), chip.sem("ff_dn_loaded"), chip.sem("ff_dn_scaled")
        raw_loaded, cleared, scaled = chip.sem("ff_raw_loaded"), chip.sem("ff_cleared"), chip.sem("ff_scaled")
        rows_loaded, tail_cleared, turned = chip.sem("ff_rows_loaded"), chip.sem("ff_tail"), chip.sem("ff_turned")
        summed, sig_ready, hid_step = chip.sem("ff_summed"), chip.sem("ff_sig"), chip.sem("ff_hid_steps")
        hid_ready, h_hi_ready, h_lo_ready = chip.sem("ff_hid"), chip.sem("ff_h_hi"), chip.sem("ff_h_lo")
        taken, squared, mean_ready = chip.sem("ff_y"), chip.sem("ff_squared"), chip.sem("ff_mean")
        root_ready, norm_step = chip.sem("ff_root"), chip.sem("ff_norm_steps")
        out_ready, stored = chip.sem("ff_out"), chip.sem("ff_stored")
        block = ctx.enter_context(nc.Block())

        def each_block(eng, body):
            with eng.Fori(0, NB - 1) as b:
                body(b, False)
            body(NB - 1, True)

        @block.sync
        def _(sp):
            def load(b, parts):
                for g in range(2):
                    src = gu_d[bass.ds(b * D + g * INNER, WORD * parts), :].rearrange("(w j) c -> w j c", j=WORD)
                    sp.dma_start(rows[g][0:parts], src).then_inc(rows_loaded, 16)

            for k in range(WORD):
                sp.dma_start(raw[k * GROUP_ROWS:(k + 1) * GROUP_ROWS, :],
                             gu_scale_d[k].rearrange("(a n) -> a n", a=1).to_broadcast((GROUP_ROWS, 2 * INNER)))\
                    .then_inc(raw_loaded, 16)
            load(0, P)
            sp.wait_ge(dn_cleared, 2)
            sp.dma_start(dn_rows[:, :, 0:INNER // WORD], dn_d.rearrange("(a p) c -> p a c", p=P)).then_inc(dn_loaded, 16)
            for k in range(INNER // P):
                b, at = k // 8, (k % 8) * GROUP_ROWS
                sp.dma_start(dn_scale[at:at + GROUP_ROWS, b, :],
                             dn_scale_d[k].rearrange("(a n) -> a n", a=1).to_broadcast((GROUP_ROWS, D)))\
                    .then_inc(dn_loaded, 16)
            sp.wait_ge(turned, 2 * NQ)
            load(1, P)
            sp.wait_ge(tail_cleared, 2)
            load(NB - 1, LAST)
            for t in range(T):
                sp.wait_ge(out_ready, t + 1)
                sp.dma_start(out_d[t], y[:, t, :]).then_inc(stored, 16)
            sp.wait_ge(stored, 16 * T)

        @block.tensor
        def _(pe):
            pe.sem_inc(summed, SUMMED0)

            def turn_words(c, source, first=False):
                for g in range(2):
                    if not first:
                        pe.wait_ge(unpack.taken, 2 * c + g - 1)
                    for j in range(QC):
                        last = nc.tensor.transpose(turn[g][:, j * P:(j + 1) * P], source(g, j).bitcast(F32), ident32[:])
                    last.then_inc(turned, 1)

            def turn_rows_of(c, b, q, first=False):
                if q == 0:
                    pe.wait_ge(rows_loaded, 32 * b + 32)
                turn_words(c, lambda g, j: rows[g][:, QC * q + j, :], first)

            def turn_down(m):
                half, b = down[m]
                if m == 0:
                    pe.wait_ge(dn_loaded, 16 * (1 + INNER // P))
                turn_words(NUP + m, lambda g, j: dn_rows[:, 4 * half + QC * g + j, b * P:(b + 1) * P])

            def body(b, last_block):
                for q in range(NQ):
                    c = NQ * b + q
                    if q + 1 < NQ:
                        turn_rows_of(c + 1, b, q + 1)
                    elif not last_block:
                        turn_rows_of(c + 1, b + 1, 0)
                    else:
                        turn_down(0)
                    unpack.wait(pe, c)
                    for j in range(QC):
                        pe.wait_ge(hid_ready, HID0 + QC * (c - 1) + j + 1)
                        for g in range(2):
                            cols = slice(g * COLS + j * P, g * COLS + (j + 1) * P)
                            for k in range(WORD):
                                for n, (w, v) in enumerate(((w_hi, xt_hi), (w_hi, xt_lo), (w_lo, xt_hi))):
                                    last = nc.tensor.matmul(acc[j][g][:], w[q % 2][:, k, cols], v[:, k, :],
                                                            start=(k == 0 and n == 0),
                                                            stop=(k == WORD - 1 and n == 2))
                        last.then_inc(summed, 1)

            turner.tensor(pe)
            turn_rows_of(0, 0, 0, True)
            turner.wait_tile(pe, T - 1)
            each_block(pe, body)
            for m, (half, b) in enumerate(down):
                if m + 1 < len(down):
                    turn_down(m + 1)
                unpack.wait(pe, NUP + m)
                if m == 0:
                    pe.wait_ge(hid_ready, HID0 + NB * WORD)
                    pe.wait_ge(h_lo_ready, HLO0 + NB * WORD)
                for t in range(T):
                    if half == 1 and b == 0:
                        pe.wait_ge(taken, t + 1)
                    for k in range(WORD):
                        for n, (v, w) in enumerate(((h_hi, w_hi), (h_hi, w_lo), (h_lo, w_hi))):
                            last = nc.tensor.matmul(dn_acc[t][:], v[:, b * WORD + k, t * P:(t + 1) * P], w[m % 2][:, k, :],
                                                    start=(b == 0 and k == 0 and n == 0),
                                                    stop=(b == NB - 1 and k == WORD - 1 and n == 2))
                    last.then_inc(summed, 1)

        @block.vector
        def _(dve):
            dve.sem_inc(hid_ready, HID0)
            turner.vector(dve)
            def products(c):
                if c < NUP:
                    b, q = c // NQ, c % NQ
                    if q == 0:
                        dve.wait_ge(scaled, 2 * (b + 1))
                    scales = [scale[:, g * NB + b, QC * q:QC * q + QC, :].rearrange("p j w -> p (j w)")
                              for g in range(2)]
                else:
                    half, b = down[c - NUP]
                    scales = [dn_scale[:, b, half * HALF + g * COLS:half * HALF + (g + 1) * COLS] for g in range(2)]
                unpack.products(dve, c, turned, words, scales)

            def low(c, g=1):
                cols = slice(g * COLS, (g + 1) * COLS)
                unpack.low(dve, nc.vector, c, g, w_hi[c % 2][:, :, cols], w_lo[c % 2][:, :, cols])

            def hidden(c, j):
                dve.wait_ge(sig_ready, QC * c + j + 1)
                nc.vector.scalar_tensor_tensor(out=sig[j][:], in0=acc[j][0][:], scalar=UP_OUT, in1=sig[j][:],
                                               op0=ALU.mult, op1=ALU.mult).then_inc(hid_step, 1)
                dve.wait_ge(hid_step, QC * c + j + 1)
                dve.wait_ge(h_lo_ready, HLO0 + QC * (c - 1) + j + 1)
                nc.vector.scalar_tensor_tensor(out=hid[j][:], in0=acc[j][1][:], scalar=UP_OUT * H_SCALE,
                                               in1=sig[j][:], op0=ALU.mult, op1=ALU.mult).then_inc(hid_ready, 1)

            products(0)
            low(0, 0)
            low(0)
            for c in range(NUP):
                if c + 1 == NUP:
                    dve.wait_ge(dn_scaled, 1)
                products(c + 1)
                if c + 2 == NQ * (NB - 1):
                    dve.wait_ge(turned, 2 * NQ * (NB - 1))
                    for g in range(2):
                        nc.vector.memset(rows[g][LAST:P], 0).then_inc(tail_cleared, 1)
                for j in range(QC):
                    hidden(c, j)
                    if j == 0:
                        low(c + 1)
            for m, (half, b) in enumerate(down):
                if m + 1 < len(down):
                    products(NUP + m + 1)
                    low(NUP + m + 1)
                if b == NB - 1:
                    for t in range(T):
                        dve.wait_ge(summed, UP_SUMMED + T * m + t + 1)
                        nc.vector.tensor_scalar(y[:, t, half * HALF:(half + 1) * HALF], dn_acc[t][:], DOWN_OUT, None,
                                                ALU.mult).then_inc(taken, 1)
            dve.wait_ge(squared, T)
            var, root, tmp, rstd = (small[:, k, :] for k in range(1, 5))
            nc.vector.tensor_scalar(var, small[:, 0, :], 1.0 / D, RMS_EPS, ALU.mult, ALU.add).then_inc(mean_ready, 1)
            dve.wait_ge(mean_ready, 1)
            rsqrt_steps(nc, dve, norm_step, 0, root_ready, 1, var, root, tmp, rstd)
            for t in range(T):
                nc.vector.scalar_tensor_tensor(out=y[:, t, :], in0=y[:, t, :], scalar=rstd[:, t:t + 1],
                                               in1=x[:, t, :], op0=ALU.mult, op1=ALU.add).then_inc(out_ready, 1)

        @block.scalar
        def _(act):
            def high(c, j, used):
                for g in range(2):
                    act.wait_ge(summed, used)
                    unpack.high(act, 2 * c + g, g, w_hi[j][:, :, g * COLS:(g + 1) * COLS])

            def hidden(b, q, j):
                c = NQ * b + q
                act.wait_ge(summed, SUMMED0 + QC * c + j + 1)
                act.wait_ge(hid_ready, HID0 + QC * (c - 1) + j + 1)
                nc.scalar.activation(sig[j][:], acc[j][0][:], ACT.Sigmoid, scale=UP_OUT).then_inc(sig_ready, 1)
                act.wait_ge(hid_ready, HID0 + QC * c + j + 1)
                nc.scalar.activation(h_hi[:, bass.ds(b * WORD + QC * q + j, 1), :].rearrange("p a n -> p (a n)"),
                                     hid[j][:], ACT.Copy).then_inc(h_hi_ready, 1)

            def body(b, last_block):
                for q in range(NQ):
                    c = NQ * b + q
                    high(c + 1, (q + 1) % 2, SUMMED0 + QC * c)
                    for j in range(QC):
                        hidden(b, q, j)

            turner.scalar(act)
            act.wait_ge(cleared, 1)
            act.wait_ge(raw_loaded, 16 * WORD)
            for b in range(NB):
                for g in range(2):
                    n = P if b < NB - 1 else LAST
                    at = g * INNER + b * D
                    nc.scalar.activation(scale[:, g * NB + b, :, 0:n],
                                         raw[:, at:at + WORD * n].rearrange("p (w j) -> p j w", j=WORD),
                                         ACT.Copy, scale=SC_SCALE).then_inc(scaled, 1)
                if b == 0:
                    high(0, 0, SUMMED0 - QC)
            each_block(act, body)
            for m in range(1, len(down)):
                high(NUP + m, m % 2, UP_SUMMED + T * (m - 1))
            for t in range(T):
                act.wait_ge(taken, T + t + 1)
                if t:
                    act.wait_ge(squared, t)
                nc.scalar.activation(sq, y[:, t, :], ACT.Square, accum_out=small[:, 0, t:t + 1]).then_inc(squared, 1)
            act.wait_ge(mean_ready, 1)
            nc.scalar.activation(small[:, 2, :], small[:, 1, :], ACT.Sqrt).then_inc(root_ready, 1)

        @block.gpsimd
        def _(pool):
            pool.sem_inc(h_lo_ready, HLO0)

            nc.gpsimd.memset(scale[:].rearrange("p b j w -> p (b j w)").bitcast(I32), 0).then_inc(cleared, 1)
            nc.gpsimd.memset(dn_rows[:], 0).then_inc(dn_cleared, 1)
            nc.gpsimd.memset(dn_scale[:].rearrange("p b n -> p (b n)").bitcast(I32), 0).then_inc(dn_cleared, 1)
            pool.wait_ge(dn_loaded, 16 * (1 + INNER // P))
            nc.gpsimd.tensor_scalar(dn_scale[:], dn_scale[:], SC_SCALE, None, ALU.mult).then_inc(dn_scaled, 1)

            def low(c, j):
                unpack.low(pool, nc.gpsimd, c, 0, w_hi[j][:, :, 0:COLS], w_lo[j][:, :, 0:COLS])

            def hidden(b, q, j):
                pool.wait_ge(h_hi_ready, QC * (NQ * b + q) + j + 1)
                at = bass.ds(b * WORD + QC * q + j, 1)
                nc.gpsimd.tensor_tensor(h_lo[:, at, :].rearrange("p a n -> p (a n)"), hid[j][:],
                                        h_hi[:, at, :].rearrange("p a n -> p (a n)"),
                                        ALU.subtract).then_inc(h_lo_ready, 1)

            def body(b, last_block):
                for q in range(NQ):
                    low(NQ * b + q + 1, (q + 1) % 2)
                    for j in range(QC):
                        hidden(b, q, j)

            each_block(pool, body)
            for m in range(1, len(down)):
                low(NUP + m, m % 2)


def natural(src, t, k):
    return src[:, t, k * P:(k + 1) * P]


def by_nibble(src, t, k):
    return src[:, t, :].rearrange("p (w j) -> p j w", j=WORD)[:, k, :]


def build(nc, a, out_d):
    chip = Chip(nc)
    kt_d = nc.dram_tensor("keys_turned", (HEADS, P, NKV), F16, kind="Internal").ap()
    v_d = nc.dram_tensor("values", (HEADS, P, KVT, HD), F32, kind="Internal").ap()
    scale_d = nc.dram_tensor("value_steps", (2 * D,), F32, kind="Internal").ap()
    x_d = a["x"].rearrange("b p n -> p b n")

    def halves(w):
        return [w[:, h * HALF:(h + 1) * HALF] for h in range(w.shape[1] // HALF)]

    def cols(n):
        return slice(n * HALF, (n + 1) * HALF)

    with chip.all, ExitStack() as whole:
        ident32 = chip.sb(whole, "ident32", [P, P], F32)
        ident16 = chip.sb(whole, "ident16", [P, P], F16)
        o = chip.sb(whole, "o", [P, T, D], F32)
        x = chip.sb(whole, "x", [P, T, D], F32)
        x_loaded = chip.sem("x_loaded")
        start(chip, a["ident"], ident32, ident16, x_d, x, x_loaded)
        with ExitStack() as cross:
            q_t = chip.sb(cross, "q_t", [P, HEADS, T * P], F16)
            exp_scale = chip.sb(cross, "exp_scale", [P, HEADS, T], F32)
            v_scale = chip.sb(cross, "v_scale", [P, 2, D], F32)
            twice = chip.sb(cross, "q_twice", [P, T, HEADS, 2, HD], F16)
            vmax = v_scale[:, 1, :]
            with ExitStack() as c:
                w_hi = chip.sb(c, "kv_whi", [P, 4, KD, HALF], F16)
                w_lo = chip.sb(c, "kv_wlo", [P, 4, KD, HALF], F16)
                kv_bias = chip.sb(c, "kv_bias", [P, 2 * D], F32)
                rows = [chip.sb(c, f"kv_rows{s}", [P, D], F32) for s in range(2)]
                ctx_loaded = [chip.sem(f"kv_rows_loaded{s}") for s in range(2)]
                q = o
                with ExitStack() as cc:
                    room = twice[:].rearrange("p t h c d -> p (t h c d)").rearrange("p (q k n) -> p q k n", q=2, n=HALF)
                    panels = WeightPanels(chip, cc, "wq", halves(a["wq"]) + halves(a["wkv"]),
                                          {0: (room[:, 0], room[:, 1]),
                                           **{2 + n: (w_hi[:, n], w_lo[:, n]) for n in range(4)}})
                    bias = chip.sb(cc, "q_bias", [P, D], F32)
                    xt_hi, xt_lo = q_t[:, 0:KD, :], q_t[:, KD:2 * KD, :]
                    start_loads(chip, panels, (bias[:], flat_bcast(a["bq"], D)),
                                (kv_bias[:], flat_bcast(a["bkv"], 2 * D)),
                                apart=[(rows[s][:], a["ctx"][s], ctx_loaded[s]) for s in range(2)])
                    project(chip, "pq", panels, 0, 2, (0, 1, 2), ((3, 4, 5), ()),
                            (q, natural, xt_hi, xt_lo, ident32, x, None, x_loaded),
                            lambda n, t: bias[:, cols(n)], lambda n, t: q[:, t, cols(n)])
                queries = Queries(chip, c, q, exp_scale, twice)
                stores = keys_and_values(chip, a["ctx"], rows, ctx_loaded, w_hi, w_lo, kv_bias, kt_d, v_d, vmax,
                                         ident32, ident16, queries)
            heads = HeadLoads(chip, cross, kt_d, v_d)
            value_scales(chip, vmax, scale_d, v_scale, twice, q_t, ident32, ident16, stores, heads)
            attend_quantised(chip, q_t, exp_scale, heads, v_scale, twice, o, ident16)
        stats = row_stats_of(chip, whole)
        with ExitStack() as c:
            bias = chip.sb(c, "bias", [P, 5, D], F32)
            tables = chip.sb(c, "rope_tables", [P, 2, HD], F32)
            mask = chip.sb(c, "mask", [P, P], F32)
            panels = WeightPanels(chip, c, "wt", [h for w in ("wp", "wq2", "wk2", "wv2", "wo") for h in halves(a[w])])
            start_loads(chip, panels, (bias[:, 0, :], flat_bcast(a["bp"], D)),
                        (bias[:, 1, :], flat_bcast(a["bq2"], D)), (bias[:, 2, :], flat_bcast(a["bk2"], D)),
                        (bias[:, 3, :], flat_bcast(a["bv2"], D)), (bias[:, 4, :], flat_bcast(a["bo"], D)),
                        (tables[:], a["rope"].rearrange("c p d -> p c d")), (mask[:], a["mask"]))

            def add_projection(tag, first, split_first, split_after, row):
                with ExitStack() as cc:
                    xt_hi = chip.sb(cc, f"{tag}_xthi", [P, KD, T * P], F16)
                    xt_lo = chip.sb(cc, f"{tag}_xtlo", [P, KD, T * P], F16)
                    project(chip, tag, panels, first, 2, split_first, split_after,
                            (o, natural, xt_hi, xt_lo, ident32), lambda n, t: x[:, t, cols(n)],
                            lambda n, t: x[:, t, cols(n)], added=(x, bias[:, row, :]), stats=(stats, x))

            add_projection("pp", 0, (0, 1), ((2,), ()), 0)
            with ExitStack() as cc:
                y = [chip.sb(cc, f"y{w}", [P, T, D], F32) for w in range(3)]
                with ExitStack() as ccc:
                    xt_hi = chip.sb(ccc, "s_xthi", [P, KD, T * P], F16)
                    xt_lo = chip.sb(ccc, "s_xtlo", [P, KD, T * P], F16)
                    swapped = chip.sb(ccc, "rope_swapped", [P, T, HEADS, HD], F32)
                    rope_step = chip.sem("rope_steps")

                    def rotate_both(pool):
                        steps = 0
                        for w in range(2):
                            pool.wait_ge(panels.taken, T * (2 + 2 * w + 2))
                            steps = rotate(nc, pool, y[w], rope_step, steps, tables[:, 0, :], tables[:, 1, :], swapped)

                    project(chip, "ps", panels, 2, 6, (3,), ((4,), (5,), (6,), (7,), (8,), ()),
                            (o, natural, xt_hi, xt_lo, ident32, x, stats), lambda n, t: bias[:, 1 + n // 2, cols(n % 2)],
                            lambda n, t: y[n // 2][:, t, cols(n % 2)], beside=rotate_both)
                attend_causal(chip, y[0], y[1], y[2], mask, o, ident32)
            add_projection("po", 8, (9,), ((), ()), 4)
        with ExitStack() as c:
            xt_hi = chip.sb(c, "f_xthi", [P, KD, T * P], F16)
            xt_lo = chip.sb(c, "f_xtlo", [P, KD, T * P], F16)
            feed_forward(chip, (o, by_nibble, xt_hi, xt_lo, ident32, x, stats), xt_hi, xt_lo, a["gu"], a["gu_scale"],
                         a["dn"], a["dn_scale"], x, o, out_d, ident32)


def kernel(x, ctx_2048, L0_xattn_Wq, L0_xattn_bq, L0_xattn_Wkv, L0_xattn_bkv, L0_xattn_Wp, L0_xattn_bp,
           L0_attn_Wq, L0_attn_bq, L0_attn_Wk, L0_attn_bk, L0_attn_Wv, L0_attn_bv, L0_attn_Wo, L0_attn_bo,
           L0_ffn_gate_up_packed, L0_ffn_gate_up_scales, L0_ffn_down_packed, L0_ffn_down_scales):
    import concourse.bacc as bacc
    from concourse.bass_utils import run_bass_kernel_spmd

    pos = np.arange(S, dtype=np.float32)[:, None]
    exps = -np.arange(0, HD, 2, dtype=np.float32) / np.float32(HD)
    angles = pos * np.repeat(np.power(np.float32(10000.0), exps), 2)[None, :]
    cos, sin = np.cos(angles), np.sin(angles)
    sin[:, 0::2] *= -1.0
    mask = np.where(np.triu(np.ones((S, S), bool), k=1), np.float32(-1e30), np.float32(0.0)).astype(np.float32)
    arrays = {
        "x": np.asarray(x), "ctx": np.asarray(ctx_2048).reshape(KVT, P, D),
        "wq": np.asarray(L0_xattn_Wq), "bq": np.asarray(L0_xattn_bq),
        "wkv": np.asarray(L0_xattn_Wkv), "bkv": np.asarray(L0_xattn_bkv),
        "wp": np.asarray(L0_xattn_Wp), "bp": np.asarray(L0_xattn_bp),
        "wq2": np.asarray(L0_attn_Wq), "wk2": np.asarray(L0_attn_Wk), "wv2": np.asarray(L0_attn_Wv),
        "bq2": np.asarray(L0_attn_bq), "bk2": np.asarray(L0_attn_bk), "bv2": np.asarray(L0_attn_bv),
        "wo": np.asarray(L0_attn_Wo), "bo": np.asarray(L0_attn_bo),
        "gu": np.asarray(L0_ffn_gate_up_packed), "gu_scale": np.asarray(L0_ffn_gate_up_scales),
        "dn": np.asarray(L0_ffn_down_packed), "dn_scale": np.asarray(L0_ffn_down_scales),
        "rope": np.stack([cos, sin]).astype(np.float32), "mask": mask, "ident": np.eye(P, dtype=np.float32),
    }
    nc = bacc.Bacc("TRN2", target_bir_lowering=False, num_devices=1)
    feeds, aps = {}, {}
    for name, v in arrays.items():
        feeds[f"in_{name}"] = v = np.ascontiguousarray(v)
        aps[name] = nc.dram_tensor(f"in_{name}", v.shape, mybir.dt.from_np(v.dtype), kind="ExternalInput").ap()
    out_d = nc.dram_tensor("out", (B, S, D), F32, kind="ExternalOutput").ap()
    build(nc, aps, out_d)
    r = run_bass_kernel_spmd(nc, [feeds], core_ids=[0])
    return r.results[0]["out"]
```
